# Optimizing a Trainium2 kernel written in Bass

```python
import numpy as np
import jax
import jax.numpy as jnp

def _softmax(x, axis=-1):
    return jax.nn.softmax(x, axis=axis)

def _gelu(x):
    return jax.nn.gelu(x, approximate=True)

def _silu(x):
    return jax.nn.silu(x)

def _sigmoid(x):
    return jax.nn.sigmoid(x)

def _layernorm(x, axis=-1, eps=1e-05):
    m = jnp.mean(x, axis=axis, keepdims=True)
    v = jnp.var(x, axis=axis, keepdims=True)
    return (x - m) / jnp.sqrt(v + eps)

def _scatter_add(tgt, idx, src, axis=0):
    return tgt.at[idx].add(src)

def _segment_sum(src, seg, n):
    return jax.ops.segment_sum(src, seg, n)
kernel_name = 'mk_gnn_ffn_d1_gnn_r8_00e812'

def setup_inputs(seed: int=0):
    np.random.seed(seed)
    _w = jnp.asarray

    def _rec_inputs():
        import jax
        import jax.numpy as jnp
        _gk = jax.random.key(seed)
        x = -0.0002117 + 1 * jax.random.normal(jax.random.fold_in(_gk, 1), (12500, 256), jnp.float32)
        _s = jax.random.randint(jax.random.fold_in(_gk, 2), (100000,), 0, 12500, jnp.int32)
        _d = jax.random.randint(jax.random.fold_in(_gk, 3), (100000,), 0, 12500, jnp.int32)
        _loop = jnp.arange(12500, dtype=jnp.int32)
        src = jnp.concatenate([_s, _d, _loop])
        dst = jnp.concatenate([_d, _s, _loop])
        _o = jnp.argsort(dst, stable=True)
        src = src[_o]
        dst = dst[_o]
        edge_weight = jax.random.uniform(jax.random.fold_in(_gk, 12), (212500,), jnp.float32, 0.0, 1)
        return (x, src, dst, edge_weight)
    x, src, dst, edge_weight = _rec_inputs()

    def _L0_gnn_setup():
        import jax, jax.numpy as jnp
        import numpy as np
        N = 12500
        D_IN = 256
        D_OUT = 256
        E = 400000
        key = jax.random.key(seed)
        ks = jax.random.split(key, 9)
        x = jax.random.normal(ks[0], (N, D_IN), dtype=jnp.float32)
        edge_src = jax.random.randint(ks[1], (E,), 0, N, dtype=jnp.int32)
        edge_dst = jax.random.randint(ks[2], (E,), 0, N, dtype=jnp.int32)
        edge_weight = jax.random.uniform(ks[3], (E,), dtype=jnp.float32)
        eps = jnp.zeros((1,), dtype=jnp.float32)
        lim1 = 1.0 / np.sqrt(D_IN)
        w1 = jax.random.uniform(ks[4], (D_IN, D_OUT), minval=-lim1, maxval=lim1, dtype=jnp.float32)
        b1 = jax.random.uniform(ks[5], (D_OUT,), minval=-lim1, maxval=lim1, dtype=jnp.float32)
        lim2 = 1.0 / np.sqrt(D_OUT)
        w2 = jax.random.uniform(ks[6], (D_OUT, D_OUT), minval=-lim2, maxval=lim2, dtype=jnp.float32)
        b2 = jax.random.uniform(ks[7], (D_OUT,), minval=-lim2, maxval=lim2, dtype=jnp.float32)
        return {'x': x, 'edge_src': edge_src, 'edge_dst': edge_dst, 'edge_weight': edge_weight, 'eps': eps, 'w1': w1, 'b1': b1, 'w2': w2, 'b2': b2}
    _L0_gnn_all = _L0_gnn_setup()
    _L0_gnn_in = {k: v for k, v in _L0_gnn_all.items() if k in ('eps', 'w1', 'b1', 'w2', 'b2')}
    del _L0_gnn_all

    def _L0_ffn_setup():
        import jax, jax.numpy as jnp
        import numpy as np
        B, A = (512, 8)
        IN, OUT = (256, 256)
        SH1, SH2 = (256, 128)
        EH1, EH2 = (128, 64)
        E, TOPK = (4, 2)

        def _shared_mlp(x, W1, b1, W2, b2, W3, b3):
            h = jax.nn.relu(x @ W1 + b1)
            h = jax.nn.relu(h @ W2 + b2)
            return h @ W3 + b3

        def _experts_mlp(x, eW1, eb1, eW2, eb2, eW3, eb3):
            h = jax.nn.relu(jnp.einsum('baf,efh->ebah', x, eW1) + eb1[:, None, None, :])
            h = jax.nn.relu(jnp.einsum('ebah,ehg->ebag', h, eW2) + eb2[:, None, None, :])
            o = jnp.einsum('ebag,ego->ebao', h, eW3) + eb3[:, None, None, :]
            return jnp.moveaxis(o, 0, -1)
        key = jax.random.key(seed)
        ks = jax.random.split(key, 16)
        s = 0.05
        return {'x': jax.random.normal(ks[0], (B, A, IN), jnp.float32), 'sW1': jax.random.normal(ks[1], (IN, SH1), jnp.float32) * s, 'sb1': jnp.zeros((SH1,), jnp.float32), 'sW2': jax.random.normal(ks[2], (SH1, SH2), jnp.float32) * s, 'sb2': jnp.zeros((SH2,), jnp.float32), 'sW3': jax.random.normal(ks[3], (SH2, OUT), jnp.float32) * s, 'sb3': jnp.zeros((OUT,), jnp.float32), 'eW1': jax.random.normal(ks[4], (E, IN, EH1), jnp.float32) * s, 'eb1': jnp.zeros((E, EH1), jnp.float32), 'eW2': jax.random.normal(ks[5], (E, EH1, EH2), jnp.float32) * s, 'eb2': jnp.zeros((E, EH2), jnp.float32), 'eW3': jax.random.normal(ks[6], (E, EH2, OUT), jnp.float32) * s, 'eb3': jnp.zeros((E, OUT), jnp.float32), 'gW': jax.random.normal(ks[7], (IN, E), jnp.float32) * s, 'gb': jnp.zeros((E,), jnp.float32)}
    _L0_ffn_all = _L0_ffn_setup()
    _L0_ffn_in = {k: v for k, v in _L0_ffn_all.items() if k in ('sW1', 'sb1', 'sW2', 'sb2', 'sW3', 'sb3', 'eW1', 'eb1', 'eW2', 'eb2', 'eW3', 'eb3', 'gW', 'gb')}
    del _L0_ffn_all
    return {'x': x, 'src': src, 'dst': dst, 'edge_weight': edge_weight, 'L0_gnn_eps': _L0_gnn_in['eps'], 'L0_gnn_w1': _L0_gnn_in['w1'], 'L0_gnn_b1': _L0_gnn_in['b1'], 'L0_gnn_w2': _L0_gnn_in['w2'], 'L0_gnn_b2': _L0_gnn_in['b2'], 'L0_ffn_sW1': _L0_ffn_in['sW1'], 'L0_ffn_sb1': _L0_ffn_in['sb1'], 'L0_ffn_sW2': _L0_ffn_in['sW2'], 'L0_ffn_sb2': _L0_ffn_in['sb2'], 'L0_ffn_sW3': _L0_ffn_in['sW3'], 'L0_ffn_sb3': _L0_ffn_in['sb3'], 'L0_ffn_eW1': _L0_ffn_in['eW1'], 'L0_ffn_eb1': _L0_ffn_in['eb1'], 'L0_ffn_eW2': _L0_ffn_in['eW2'], 'L0_ffn_eb2': _L0_ffn_in['eb2'], 'L0_ffn_eW3': _L0_ffn_in['eW3'], 'L0_ffn_eb3': _L0_ffn_in['eb3'], 'L0_ffn_gW': _L0_ffn_in['gW'], 'L0_ffn_gb': _L0_ffn_in['gb']}

def reference(x, src, dst, edge_weight, L0_gnn_eps, L0_gnn_w1, L0_gnn_b1, L0_gnn_w2, L0_gnn_b2, L0_ffn_sW1, L0_ffn_sb1, L0_ffn_sW2, L0_ffn_sb2, L0_ffn_sW3, L0_ffn_sb3, L0_ffn_eW1, L0_ffn_eb1, L0_ffn_eW2, L0_ffn_eb2, L0_ffn_eW3, L0_ffn_eb3, L0_ffn_gW, L0_ffn_gb):
    import jax
    import jax.numpy as jnp

    def _L0_gnn_ref(x, edge_src, edge_dst, edge_weight, eps, w1, b1, w2, b2):
        import jax, jax.numpy as jnp
        import numpy as np
        N = 12500
        D_IN = 256
        D_OUT = 256
        E = 400000
        msgs = edge_weight[:, None] * x[edge_src]
        agg = jax.ops.segment_sum(msgs, edge_dst, num_segments=N)
        h = (1.0 + eps[0]) * x + agg
        h = jax.nn.relu(h @ w1 + b1)
        return h @ w2 + b2

    def _L0_ffn_ref(x, sW1, sb1, sW2, sb2, sW3, sb3, eW1, eb1, eW2, eb2, eW3, eb3, gW, gb):
        import jax, jax.numpy as jnp
        import numpy as np
        B, A = (512, 8)
        IN, OUT = (256, 256)
        SH1, SH2 = (256, 128)
        EH1, EH2 = (128, 64)
        E, TOPK = (4, 2)

        def _shared_mlp(x, W1, b1, W2, b2, W3, b3):
            h = jax.nn.relu(x @ W1 + b1)
            h = jax.nn.relu(h @ W2 + b2)
            return h @ W3 + b3

        def _experts_mlp(x, eW1, eb1, eW2, eb2, eW3, eb3):
            h = jax.nn.relu(jnp.einsum('baf,efh->ebah', x, eW1) + eb1[:, None, None, :])
            h = jax.nn.relu(jnp.einsum('ebah,ehg->ebag', h, eW2) + eb2[:, None, None, :])
            o = jnp.einsum('ebag,ego->ebao', h, eW3) + eb3[:, None, None, :]
            return jnp.moveaxis(o, 0, -1)
        all_out = _experts_mlp(x, eW1, eb1, eW2, eb2, eW3, eb3)
        shared = _shared_mlp(x, sW1, sb1, sW2, sb2, sW3, sb3)
        gates = jax.nn.softmax(x @ gW + gb, axis=-1)
        topv, topi = jax.lax.top_k(gates, TOPK)
        topw = jax.nn.softmax(topv, axis=-1)
        sel = jnp.take_along_axis(all_out, topi[:, :, None, :], axis=-1)
        gated = jnp.sum(sel * topw[:, :, None, :], axis=-1)
        return shared + gated
    x = x + _L0_gnn_ref(_layernorm(x, axis=-1), src, dst, edge_weight, L0_gnn_eps, L0_gnn_w1, L0_gnn_b1, L0_gnn_w2, L0_gnn_b2)
    x = x + _L0_ffn_ref(_layernorm(x, axis=-1)[None], L0_ffn_sW1, L0_ffn_sb1, L0_ffn_sW2, L0_ffn_sb2, L0_ffn_sW3, L0_ffn_sb3, L0_ffn_eW1, L0_ffn_eb1, L0_ffn_eW2, L0_ffn_eb2, L0_ffn_eW3, L0_ffn_eb3, L0_ffn_gW, L0_ffn_gb)[0]
    return x

_drawn_inputs = setup_inputs


def setup_inputs(seed=0):
    import zlib

    import numpy as np

    out = dict(_drawn_inputs(seed))
    spreads = {'L0_ffn_sb1': (0.0, 0.495),
     'L0_ffn_sb2': (0.0, 0.1),
     'L0_ffn_sb3': (0.0, 0.1),
     'L0_ffn_eb1': (0.0, 0.8),
     'L0_ffn_eb2': (0.0, 0.586),
     'L0_ffn_eb3': (0.0, 0.1),
     'L0_ffn_gb': (0.0, 0.476)}
    factors = {'L0_gnn_b1': 4.238}
    for name, (base, spread) in spreads.items():
        noise = np.random.default_rng([zlib.crc32(name.encode()), seed]).standard_normal(out[name].shape)
        drawn = base * np.exp(spread * noise) if base else spread * noise
        out[name] = jnp.asarray(drawn.astype(out[name].dtype))
    for name, factor in factors.items():
        out[name] = (out[name] * factor).astype(out[name].dtype)
    return out
```

```python
from contextlib import ExitStack

import concourse.bass as bass
from concourse import mybir

ALU = mybir.AluOpType
ACT = mybir.ActivationFunctionType
F32 = mybir.dt.float32
I32 = mybir.dt.int32
AX_X = mybir.AxisListType.X

P = 128
D = 256
KD = D // P
WIN = 64
GROUPS = 3
NE = 4
EH1, EH2 = 128, 64
SH2 = 128
TOPK = 2
LN_EPS = 1e-5
LAG = 2
CHAIN = 4
PEEL = 3


def group_tiles(tiles):
    return [(tiles + GROUPS - 1 - g) // GROUPS for g in range(GROUPS)]


def weight_columns():
    at, out = 0, {}
    for name, width in (("w1", KD * D), ("w2", KD * D), ("sW1", KD * D), ("sW2", KD * SH2), ("sW3", D),
                        ("eW1", KD * NE * EH1), ("eW2", NE * EH2), ("eW3", KD * D), ("gW", KD * NE),
                        ("b1", KD), ("sb1", KD), ("sb2", 1), ("eb1", NE), ("eps", 1)):
        out[name] = (at, width)
        at += width
    return out, at


def build(nc, x, src, dst, weight, base, packed, rows_packed, out):
    T = x.shape[0] // P
    KT = src.shape[1]
    KG = group_tiles(KT)
    K0 = [sum(KG[:g]) for g in range(GROUPS)]
    KMAX = max(KG)
    NPAD = T * P + WIN
    NWIN = T * P // WIN
    COLS, WCOLS = weight_columns()
    assert T % 2 == 0 and T // 2 > PEEL

    with ExitStack() as ctx:
        def sb(name, shape, dt=F32):
            return ctx.enter_context(nc.sbuf_tensor(name, shape, dt))

        def bank(name):
            return ctx.enter_context(nc.psum_tensor(name, [P, 512], F32))

        def sem(name):
            return ctx.enter_context(nc.semaphore(name))

        agg = sb("agg", [P, KD, NPAD])
        idx = sb("idx", [P, 2, KT], I32)
        rows = sb("rows", [P, 2, KT, D])
        dst_i = sb("dst_i", [P, T, KT], I32)
        rel = dst_i[:].bitcast(F32)
        wts = sb("wts", [P, T * KT])
        base_i = sb("base_i", [P, T * GROUPS], I32)
        prog = sb("prog", [P, T, GROUPS])
        relc = sb("relc", [P, 2, KT])
        sel = sb("sel", [P, GROUPS, KMAX, WIN])
        est6 = sb("est6", [P, KMAX, 6])
        ework = sb("ework", [P, KMAX, 5])
        evar = sb("evar", [P, 2 * GROUPS, KMAX])
        enmean = sb("enmean", [P, 2 * GROUPS, KMAX])
        elog = sb("elog", [P, KMAX])
        einv0 = sb("einv0", [P, 2 * GROUPS, KMAX])
        einv = sb("einv", [P, KMAX])
        enewt = sb("enewt", [P, 2, KMAX])
        ewr = sb("ewr", [P, GROUPS, KMAX])
        wpk = sb("wpk", [P, WCOLS])
        rpk = sb("rpk", [NE + 1, 3 * D + NE])
        xt = sb("xt", [P, 2, D])
        x2 = sb("x2", [P, 2, D])
        y = sb("y", [P, 2, D])
        xe = sb("xe", [P, D])
        hT = sb("hT", [P, KD, P])
        a1T = sb("a1T", [P, KD, P])
        xn2 = sb("xn2", [P, D])
        xn2T = sb("xn2T", [P, KD, P])
        s1T = sb("s1T", [P, KD, P])
        s2T = sb("s2T", [P, 2, P])
        e1T = sb("e1T", [P, NE, P])
        h2 = sb("h2", [P, D])
        h2T = sb("h2T", [P, KD, P])
        topwT = sb("topwT", [NE + 1, P])
        st6 = [sb(f"st6_{n}", [P, 1, 6]) for n in range(2)]
        nwork = [sb(f"nwork_{n}", [P, 1, 5]) for n in range(2)]
        nmean = [sb(f"nmean_{n}", [P, 2]) for n in range(2)]
        var = [sb(f"var_{n}", [P, 2]) for n in range(2)]
        lnv = [sb(f"lnv_{n}", [P, 1]) for n in range(2)]
        inv0 = [sb(f"inv0_{n}", [P, 2]) for n in range(2)]
        newt = [sb(f"newt_{n}", [P, 2]) for n in range(2)]
        inv = [sb(f"inv_{n}", [P, 2]) for n in range(2)]
        gmax = sb("gmax", [P, 2])
        gex = sb("gex", [P, NE])
        gsum = sb("gsum", [P, 4])
        gp = sb("gp", [P, NE])
        gex2 = sb("gex2", [P, NE])
        gcmp = sb("gcmp", [P, 3, NE, NE])
        grank = sb("grank", [P, NE])
        gkeep = sb("gkeep", [P, NE])
        topw = sb("topw", [P, NE])
        ident = sb("ident", [P, P])
        onerow = sb("onerow", [1, P])
        eps1 = sb("eps1", [P, 1])
        iota_i = sb("iota_i", [P, WIN], I32)
        iota_f = sb("iota_f", [P, WIN])
        lim_i = sb("lim_i", [P, T, GROUPS], I32)
        before = sb("before", [P, NE, NE])
        bad = sb("bad", [P, 4])
        badmax = sb("badmax", [1, 1])
        ordered = sb("ordered", [1, 1], I32)
        far = sb("far", [P, KMAX])

        p_agg = [bank(f"p_agg{n}") for n in range(2)]
        p_A = bank("p_A")
        p_B = bank("p_B")
        p_C = bank("p_C")
        p_D = bank("p_D")
        p_E = bank("p_E")
        p_F = bank("p_F")
        l2_out, ffn_out = p_A[:, 0:D], p_A[:, D:2 * D]
        s1_out, logits = p_B[:, 0:D], p_B[:, D:D + NE]
        xeT_out, e2_out = p_D[:, 0:D], p_D[:, D:2 * D]
        h2T_out, topwT_out, s2_out = p_E[:, 0:D], p_E[0:NE, D:D + P], p_E[:, D + P:D + P + SH2]
        l1_out, xn2T_out = p_F[:, 0:D], p_F[:, D:2 * D]

        def w(name, *dims):
            a, n = COLS[name]
            v = wpk[:, a:a + n]
            return v.rearrange("p (k n) -> p k n", k=dims[0]) if dims else v

        w1, w2, sW1, eW3 = (w(n, KD) for n in ("w1", "w2", "sW1", "eW3"))
        sW2, gW = w("sW2", KD), w("gW", KD)
        sW3 = w("sW3")
        eW1 = w("eW1", KD * NE)
        eW2 = w("eW2", NE)
        out_bias = rpk[:, 0:D]
        b2_row, eb2_row, gb_row = rpk[0:1, D:2 * D], rpk[0:1, 2 * D:3 * D], rpk[0:1, 3 * D:3 * D + NE]

        idx_landed = [sem(f"idx_landed{n}") for n in range(2)]
        rows_landed = [sem(f"rows_landed{n}") for n in range(2 * GROUPS)]
        x_landed = [sem(f"x_landed{n}") for n in range(2)]
        out_stored = [sem(f"out_stored{n}") for n in range(2)]
        dst_landed, base_landed = sem("dst_landed"), sem("base_landed")
        weights_landed, wts_landed = sem("weights_landed"), sem("wts_landed")
        rows_turn = sem("rows_turn")
        const_step, ident_ready, iota_ready = sem("const_step"), sem("ident_ready"), sem("iota_ready")
        bad_ready, bad_turned, flag_ready = sem("bad_ready"), sem("bad_turned"), sem("flag_ready")
        dve_const, agg_zeroed = sem("dve_const"), sem("agg_zeroed")
        rel_ready = sem("rel_ready")
        e_bn, e_mv, e_stats = sem("e_bn"), sem("e_mv"), sem("e_stats")
        e_log, e_inv0, centered = sem("e_log"), sem("e_inv0"), sem("centered")
        e_newton = sem("e_newton")
        sel_ready, rows_used, added = sem("sel_ready"), sem("rows_used"), sem("added")
        far_ready, g_sel_ready, g_agg_done = sem("far_ready"), sem("g_sel_ready"), sem("g_agg_done")
        n_bn, n_mv, n_stats, n_log, n_inv0 = ([sem(f"{s}_{n}") for n in range(2)]
                                              for s in ("n_bn", "n_mv", "n_stats", "n_log", "n_inv0"))
        n_newton = [sem(f"n_newton_{n}") for n in range(2)]
        n_scale = sem("n_scale")
        xe_ready, xeT_done, h_ready, l1_done, a1_ready = (sem(s) for s in ("xe_ready", "xeT_done", "h_ready", "l1_done", "a1_ready"))
        l2_done, x2_ready, xn2_ready, xn2T_done, xn2T_ready = (sem(s) for s in ("l2_done", "x2_ready", "xn2_ready", "xn2T_done", "xn2T_ready"))
        s1_done, e1_done = sem("s1_done"), sem("e1_done")
        gmax_step, gex_ready, gsoft_step = sem("gmax_step"), sem("gex_ready"), sem("gsoft_step")
        gex2_ready, gtop_step = sem("gex2_ready"), sem("gtop_step")
        s1_ready, e1_ready, s2_done, e2_done, s2_ready = (sem(s) for s in ("s1_ready", "e1_ready", "s2_done", "e2_done", "s2_ready"))
        h2_ready, h2T_done, topwT_done, h2T_ready, topwT_ready = (sem(s) for s in ("h2_ready", "h2T_done", "topwT_done", "h2T_ready", "topwT_ready"))
        ffn_done, y_ready = sem("ffn_done"), sem("y_ready")
        GSOFT, GTOP = 9, 4

        def wait(eng, s, value):
            if not isinstance(value, int) or value > 0:
                eng.wait_ge(s, value)

        class Step:

            def __init__(self, i, par):
                self.i, self.par = (i + par // 2, par % 2) if par // 2 else (i, par % 2)
                self.n = self.i * 2 + self.par

            def back(self, k):
                return Step(self.i, self.par - k)

            def live(self):
                return not isinstance(self.i, int) or 0 <= self.n < T

            def group(self, g):
                return self.n * GROUPS + g, self.par * GROUPS + g

        def before_group(st, g, k):
            j = g - k
            return (st.back(-(j // GROUPS)), j % GROUPS)

        def gather(pool, st, g):
            J, b = st.group(g)
            wait(pool, idx_landed[st.par], 16 * (st.i + 1))
            wait(pool, rows_used, J - 2 * GROUPS + 1)
            pool.sem_inc(rows_turn, 1)
            for k in range(K0[g], K0[g] + KG[g]):
                nc.gpsimd.indirect_dma_start(
                    rows[:, st.par, k, :], None, x,
                    bass.IndirectOffsetOnAxis(idx[:, st.par, k:k + 1], 0)).then_inc(rows_landed[b], 16)

        def moments(dve, st6_, work, nmean, v, steps, first):
            K = st6_.shape[1]
            halves = st6_.rearrange("p k (h s) -> p k h s", h=2)
            total, lead, square, spread = work[:, 0:K, 0:2], work[:, 0:K, 2], work[:, 0:K, 3], work[:, 0:K, 4]
            nc.vector.tensor_tensor(total, halves[:, :, 0, 1:3], halves[:, :, 1, 1:3], ALU.add)
            nc.vector.tensor_tensor(lead, halves[:, :, 0, 1], halves[:, :, 1, 1], ALU.subtract).then_inc(steps, 1)
            dve.wait_ge(steps, first + 1)
            nc.vector.tensor_scalar(nmean, total[:, :, 0], -0.5, None, ALU.mult)
            nc.vector.scalar_tensor_tensor(out=square, in0=lead, scalar=0.25, in1=lead, op0=ALU.mult, op1=ALU.mult)
            nc.vector.tensor_scalar(spread, total[:, :, 1], 1.0 / D, LN_EPS, ALU.mult, ALU.add).then_inc(steps, 1)
            dve.wait_ge(steps, first + 2)
            return nc.vector.tensor_tensor(v, square, spread, ALU.add)

        def edge_stats(dve, st, g):
            J, b = st.group(g)
            if g == 0:
                wait(dve, rows_used, J - GROUPS)
                nc.vector.tensor_copy(relc[:, st.par, :], rel.rearrange("p t k -> p (t k)")[:, bass.ds(st.n * KT, KT)]
                                      ).then_inc(rel_ready, 1)
            wait(dve, rows_landed[b], 16 * KG[g] * (st.i + 1))
            for k in range(KG[g]):
                last = nc.vector.bn_stats(est6[:, k, :], rows[:, st.par, K0[g] + k, :])
            last.then_inc(e_bn, 1)
            dve.wait_ge(e_bn, J + 1)
            moments(dve, est6[:, 0:KG[g], :], ework, enmean[:, b, 0:KG[g]], evar[:, b, 0:KG[g]], e_mv, 2 * J
                    ).then_inc(e_stats, 1)

        def edge_center(act, st, g):
            J, b = st.group(g)
            act.wait_ge(e_stats, J + 1)
            wait(act, e_inv0, J)
            nc.scalar.activation(elog[:, 0:KG[g]], evar[:, b, 0:KG[g]], ACT.Ln).then_inc(e_log, 1)
            act.wait_ge(e_log, J + 1)
            nc.scalar.activation(einv0[:, b, 0:KG[g]], elog[:, 0:KG[g]], ACT.Exp, scale=-0.5).then_inc(e_inv0, 1)
            for k in range(KG[g]):
                r = rows[:, st.par, K0[g] + k, :]
                last = nc.scalar.activation(r, r, ACT.Identity, bias=enmean[:, b, k:k + 1])
            last.then_inc(centered, 1)
            if g == GROUPS - 1:
                nxt = st.back(-2)
                nc.scalar.dma_start(idx[:, st.par, :], src[bass.ds(nxt.n * P, P), :]).then_inc(idx_landed[st.par], 16)

        def edge_scale(dve, st, g):
            J, b = st.group(g)
            K = KG[g]
            v, y0 = evar[:, b, 0:K], einv0[:, b, 0:K]
            dve.wait_ge(e_inv0, J + 1)
            wait(dve, e_newton, 4 * J)
            nc.vector.scalar_tensor_tensor(out=enewt[:, 0, 0:K], in0=y0, scalar=-0.5, in1=y0,
                                           op0=ALU.mult, op1=ALU.mult).then_inc(e_newton, 1)
            dve.wait_ge(e_newton, 4 * J + 1)
            nc.vector.tensor_tensor(enewt[:, 1, 0:K], enewt[:, 0, 0:K], v, ALU.mult).then_inc(e_newton, 1)
            dve.wait_ge(e_newton, 4 * J + 2)
            nc.vector.scalar_tensor_tensor(out=einv[:, 0:K], in0=enewt[:, 1, 0:K], scalar=1.5, in1=y0,
                                           op0=ALU.add, op1=ALU.mult).then_inc(e_newton, 1)
            dve.wait_ge(e_newton, 4 * J + 3)
            nc.vector.tensor_tensor(ewr[:, g, 0:K], einv[:, 0:K], wts[:, bass.ds(st.n * KT + K0[g], K)],
                                    ALU.mult).then_inc(e_newton, 1)
            dve.wait_ge(e_newton, 4 * J + 4)

        def edge_select(dve, st, g):
            J, b = st.group(g)
            wait(dve, rel_ready, st.n + 1)
            wait(dve, rows_used, J - GROUPS + 1)
            for k in range(KG[g]):
                last = nc.vector.tensor_scalar(sel[:, g, k, :], iota_f[:], relc[:, st.par, K0[g] + k:K0[g] + k + 1],
                                               ewr[:, g, k:k + 1], ALU.is_equal, ALU.mult)
            last.then_inc(sel_ready, 1)

        def aggregate(st, g, bank_, done):
            for c in range(KD):
                for k in range(KG[g]):
                    last = nc.tensor.matmul(bank_[:, c * WIN:(c + 1) * WIN],
                                            rows[:, st.par, K0[g] + k, c * P:(c + 1) * P], sel[:, g, k, :],
                                            start=(k == 0), stop=(k == KG[g] - 1))
            last.then_inc(done, 1)

        def edge_aggregate(pe, st, g):
            J, b = st.group(g)
            pe.wait_ge(sel_ready, J + 1)
            pe.wait_ge(centered, J + 1)
            wait(pe, added, J - 1)
            aggregate(st, g, p_agg[b % 2], rows_used)

        def edge_add(dve, st, g):
            J, b = st.group(g)
            at = dve.value_load(base_i[0:1, bass.ds(J, 1)], min_val=0, max_val=T * P)
            dve.wait_ge(rows_used, J + 1)
            wait(dve, added, J)
            a = agg[:, :, bass.ds(at, WIN)]
            nc.vector.tensor_tensor(a, p_agg[b % 2][:, 0:KD * WIN].rearrange("p (c n) -> p c n", c=KD), a,
                                    ALU.add).then_inc(added, 1)

        def norm_stats(dve, m, n, src_tile):
            nc.vector.bn_stats(st6[n][:, 0, :], src_tile).then_inc(n_bn[n], 1)
            dve.wait_ge(n_bn[n], m.n + 1)
            moments(dve, st6[n][:], nwork[n], nmean[n][:, m.par:m.par + 1], var[n][:, m.par:m.par + 1], n_mv[n],
                    2 * m.n).then_inc(n_stats[n], 1)

        def norm_inv0(act, m, n):
            act.wait_ge(n_stats[n], m.n + 1)
            wait(act, n_inv0[n], m.n)
            nc.scalar.activation(lnv[n][:], var[n][:, m.par:m.par + 1], ACT.Ln).then_inc(n_log[n], 1)
            act.wait_ge(n_log[n], m.n + 1)
            nc.scalar.activation(inv0[n][:, m.par:m.par + 1], lnv[n][:], ACT.Exp, scale=-0.5).then_inc(n_inv0[n], 1)

        def norm_inv(dve, m, n):
            v, y0 = var[n][:, m.par:m.par + 1], inv0[n][:, m.par:m.par + 1]
            dve.wait_ge(n_inv0[n], m.n + 1)
            wait(dve, n_newton[n], 3 * m.n)
            nc.vector.scalar_tensor_tensor(out=newt[n][:, 0:1], in0=y0, scalar=-0.5, in1=y0,
                                           op0=ALU.mult, op1=ALU.mult).then_inc(n_newton[n], 1)
            dve.wait_ge(n_newton[n], 3 * m.n + 1)
            nc.vector.tensor_tensor(newt[n][:, 1:2], newt[n][:, 0:1], v, ALU.mult).then_inc(n_newton[n], 1)
            dve.wait_ge(n_newton[n], 3 * m.n + 2)
            nc.vector.scalar_tensor_tensor(out=inv[n][:, 0:1], in0=newt[n][:, 1:2], scalar=1.5, in1=y0,
                                           op0=ALU.add, op1=ALU.mult).then_inc(n_newton[n], 1)
            dve.wait_ge(n_newton[n], 3 * m.n + 3)

        def d_stats1(dve, m):
            dve.wait_ge(x_landed[m.par], 16 * (m.i + 1))
            norm_stats(dve, m, 0, xt[:, m.par, :])

        def a_inv1(act, m):
            norm_inv0(act, m, 0)

        def d_xe(dve, m):
            norm_inv(dve, m, 0)
            wait(dve, dve_const, 3)
            nc.vector.tensor_tensor(inv[0][:, 1:2], inv[0][:, 0:1], eps1[:], ALU.mult).then_inc(n_scale, 1)
            dve.wait_ge(n_scale, m.n + 1)
            wait(dve, xeT_done, m.n)
            nc.vector.tensor_scalar(xe[:], xt[:, m.par, :], nmean[0][:, m.par:m.par + 1], inv[0][:, 1:2],
                                    ALU.add, ALU.mult).then_inc(xe_ready, 1)

        def p_xeT(pe, m):
            pe.wait_ge(xe_ready, m.n + 1)
            wait(pe, h_ready, m.n)
            for c in range(KD):
                last = nc.tensor.transpose(xeT_out[:, c * P:(c + 1) * P], xe[:, c * P:(c + 1) * P], ident[:])
            last.then_inc(xeT_done, 1)

        def d_h(dve, m, edges_done):
            dve.wait_ge(xeT_done, m.n + 1)
            edges_done(dve)
            wait(dve, l1_done, m.n)
            nc.vector.tensor_tensor(hT[:], xeT_out.rearrange("p (c n) -> p c n", c=KD),
                                    agg[:, :, bass.ds(m.n * P, P)], ALU.add).then_inc(h_ready, 1)

        def p_l1(pe, m):
            pe.wait_ge(h_ready, m.n + 1)
            wait(pe, a1_ready, m.n)
            for o in range(KD):
                for c in range(KD):
                    last = nc.tensor.matmul(l1_out[:, o * P:(o + 1) * P], w1[:, c, o * P:(o + 1) * P], hT[:, c, :],
                                            start=(c == 0), stop=(c == KD - 1))
            last.then_inc(l1_done, 1)

        def a_a1(act, m):
            act.wait_ge(l1_done, m.n + 1)
            wait(act, l2_done, m.n)
            b = COLS["b1"][0]
            for o in range(KD):
                last = nc.scalar.activation(a1T[:, o, :], l1_out[:, o * P:(o + 1) * P], ACT.Relu,
                                            bias=wpk[:, b + o:b + o + 1])
            last.then_inc(a1_ready, 1)

        def p_l2(pe, m):
            pe.wait_ge(a1_ready, m.n + 1)
            wait(pe, x2_ready, m.n)
            for c in range(KD):
                nc.tensor.matmul(l2_out, a1T[:, c, :], w2[:, c, :], start=(c == 0), stop=False)
            nc.tensor.matmul(l2_out, onerow[:], b2_row, start=False, stop=True).then_inc(l2_done, 1)

        def d_x2(dve, m):
            dve.wait_ge(l2_done, m.n + 1)
            wait(dve, y_ready, m.n - 1)
            nc.vector.tensor_tensor(x2[:, m.par, :], l2_out, xt[:, m.par, :], ALU.add).then_inc(x2_ready, 1)
            dve.wait_ge(x2_ready, m.n + 1)
            norm_stats(dve, m, 1, x2[:, m.par, :])

        def a_inv2(act, m):
            norm_inv0(act, m, 1)

        def d_xn2(dve, m):
            norm_inv(dve, m, 1)
            wait(dve, xn2T_done, m.n)
            nc.vector.tensor_scalar(xn2[:], x2[:, m.par, :], nmean[1][:, m.par:m.par + 1], inv[1][:, 0:1],
                                    ALU.add, ALU.mult).then_inc(xn2_ready, 1)

        def p_xn2T(pe, m):
            pe.wait_ge(xn2_ready, m.n + 1)
            wait(pe, xn2T_ready, m.n)
            for c in range(KD):
                last = nc.tensor.transpose(xn2T_out[:, c * P:(c + 1) * P], xn2[:, c * P:(c + 1) * P], ident[:])
            last.then_inc(xn2T_done, 1)

        def a_xn2T(act, m):
            act.wait_ge(xn2T_done, m.n + 1)
            wait(act, e1_done, m.n)
            nc.scalar.copy(xn2T[:].rearrange("p c n -> p (c n)"), xn2T_out).then_inc(xn2T_ready, 1)

        def p_first(pe, m):
            pe.wait_ge(xn2T_ready, m.n + 1)
            wait(pe, s1_ready, m.n)
            for c in range(KD):
                nc.tensor.matmul(logits, xn2T[:, c, :], gW[:, c, :], start=(c == 0), stop=False)
            nc.tensor.matmul(logits, onerow[:], gb_row, start=False, stop=True)
            for o in range(KD):
                for c in range(KD):
                    last = nc.tensor.matmul(s1_out[:, o * P:(o + 1) * P], sW1[:, c, o * P:(o + 1) * P], xn2T[:, c, :],
                                            start=(c == 0), stop=(c == KD - 1))
            last.then_inc(s1_done, 1)
            wait(pe, e1_ready, m.n)
            for e in range(NE):
                for c in range(KD):
                    last = nc.tensor.matmul(p_C[:, e * P:(e + 1) * P], eW1[:, c * NE + e, :], xn2T[:, c, :],
                                            start=(c == 0), stop=(c == KD - 1))
            last.then_inc(e1_done, 1)

        def d_gmax(dve, m):
            dve.wait_ge(s1_done, m.n + 1)
            nc.vector.tensor_reduce(gmax[:, 0:1], logits, AX_X, ALU.max).then_inc(gmax_step, 1)
            dve.wait_ge(gmax_step, 2 * m.n + 1)
            nc.vector.tensor_scalar(gmax[:, 1:2], gmax[:, 0:1], -1.0, None, ALU.mult).then_inc(gmax_step, 1)

        def a_first(act, m):
            act.wait_ge(gmax_step, 2 * m.n + 2)
            nc.scalar.activation(gex[:], logits, ACT.Exp, bias=gmax[:, 1:2]).then_inc(gex_ready, 1)
            act.wait_ge(s1_done, m.n + 1)
            wait(act, s2_done, m.n)
            b = COLS["sb1"][0]
            for o in range(KD):
                last = nc.scalar.activation(s1T[:, o, :], s1_out[:, o * P:(o + 1) * P], ACT.Relu,
                                            bias=wpk[:, b + o:b + o + 1])
            last.then_inc(s1_ready, 1)
            act.wait_ge(e1_done, m.n + 1)
            wait(act, e2_done, m.n)
            b = COLS["eb1"][0]
            for e in range(NE):
                last = nc.scalar.activation(e1T[:, e, :], p_C[:, e * P:(e + 1) * P], ACT.Relu,
                                            bias=wpk[:, b + e:b + e + 1])
            last.then_inc(e1_ready, 1)

        def p_second(pe, m):
            pe.wait_ge(s1_ready, m.n + 1)
            wait(pe, h2T_ready, m.n)
            for c in range(KD):
                last = nc.tensor.matmul(s2_out, sW2[:, c, :], s1T[:, c, :], start=(c == 0), stop=(c == KD - 1))
            last.then_inc(s2_done, 1)
            pe.wait_ge(e1_ready, m.n + 1)
            wait(pe, h2_ready, m.n)
            for e in range(NE):
                o = e2_out[:, e * EH2:(e + 1) * EH2]
                nc.tensor.matmul(o, e1T[:, e, :], eW2[:, e, :], start=True, stop=False)
                last = nc.tensor.matmul(o, onerow[:], eb2_row[:, e * EH2:(e + 1) * EH2], start=False, stop=True)
            last.then_inc(e2_done, 1)

        def a_s2(act, m):
            act.wait_ge(s2_done, m.n + 1)
            wait(act, ffn_done, m.n - 1)
            b = COLS["sb2"][0]
            nc.scalar.activation(s2T[:, m.par, :], s2_out, ACT.Relu, bias=wpk[:, b:b + 1]).then_inc(s2_ready, 1)

        def d_gsoft(dve, m):
            n = [GSOFT * m.n]
            by_row = gp[:].unsqueeze(1).to_broadcast([P, NE, NE])
            by_col = gp[:].unsqueeze(2).to_broadcast([P, NE, NE])

            def step(ins, after=True):
                ins.then_inc(gsoft_step, 1)
                n[0] = n[0] + 1
                dve.wait_ge(gsoft_step, n[0])

            dve.wait_ge(gex_ready, m.n + 1)
            step(nc.vector.reduce_sum(gsum[:, 0:1], gex[:], AX_X))
            step(nc.vector.reciprocal(gsum[:, 1:2], gsum[:, 0:1]))
            step(nc.vector.tensor_scalar(gp[:], gex[:], gsum[:, 1:2], None, ALU.mult))
            step(nc.vector.tensor_scalar(gsum[:, 2:3], gsum[:, 1:2], -1.0, None, ALU.mult))
            step(nc.vector.tensor_tensor(gcmp[:, 0], by_row, by_col, ALU.is_gt))
            step(nc.vector.tensor_tensor(gcmp[:, 1], by_row, by_col, ALU.is_equal))
            step(nc.vector.tensor_tensor(gcmp[:, 2], gcmp[:, 1], before[:], ALU.mult))
            step(nc.vector.tensor_tensor(gcmp[:, 1], gcmp[:, 2], gcmp[:, 0], ALU.add))
            step(nc.vector.tensor_reduce(grank[:], gcmp[:, 1], AX_X, ALU.add))

        def a_gex2(act, m):
            act.wait_ge(gsoft_step, GSOFT * m.n + 4)
            wait(act, gtop_step, GTOP * m.n)
            nc.scalar.activation(gex2[:], gp[:], ACT.Exp, bias=gsum[:, 2:3]).then_inc(gex2_ready, 1)

        def d_gtop(dve, m):
            dve.wait_ge(gex2_ready, m.n + 1)
            wait(dve, topwT_done, m.n)
            n = GTOP * m.n
            nc.vector.scalar_tensor_tensor(out=gkeep[:], in0=grank[:], scalar=TOPK - 0.5, in1=gex2[:],
                                           op0=ALU.is_lt, op1=ALU.mult).then_inc(gtop_step, 1)
            dve.wait_ge(gtop_step, n + 1)
            nc.vector.reduce_sum(gsum[:, 3:4], gkeep[:], AX_X).then_inc(gtop_step, 1)
            dve.wait_ge(gtop_step, n + 2)
            nc.vector.reciprocal(gmax[:, 0:1], gsum[:, 3:4]).then_inc(gtop_step, 1)
            dve.wait_ge(gtop_step, n + 3)
            nc.vector.tensor_scalar(topw[:], gkeep[:], gmax[:, 0:1], None, ALU.mult).then_inc(gtop_step, 1)

        def a_h2(act, m):
            act.wait_ge(e2_done, m.n + 1)
            act.wait_ge(gtop_step, GTOP * m.n + GTOP)
            wait(act, h2T_done, m.n)
            for e in range(NE):
                s = slice(e * EH2, (e + 1) * EH2)
                last = nc.scalar.activation(h2[:, s], e2_out[:, s], ACT.Relu, scale=topw[:, e:e + 1])
            last.then_inc(h2_ready, 1)

        def p_turn(pe, m):
            pe.wait_ge(gtop_step, GTOP * m.n + 4)
            pe.wait_ge(s2_ready, m.n + 1)
            nc.tensor.transpose(topwT_out, topw[:], ident[:]).then_inc(topwT_done, 1)
            pe.wait_ge(h2_ready, m.n + 1)
            for c in range(KD):
                last = nc.tensor.transpose(h2T_out[:, c * P:(c + 1) * P], h2[:, c * P:(c + 1) * P], ident[:])
            last.then_inc(h2T_done, 1)

        def a_turn(act, m):
            act.wait_ge(h2T_done, m.n + 1)
            wait(act, ffn_done, m.n)
            if isinstance(m.n, int) and m.n == 0:
                act.wait_ge(dve_const, 3)
            nc.scalar.copy(topwT[0:NE, :], topwT_out).then_inc(topwT_ready, 1)
            nc.scalar.copy(h2T[:].rearrange("p c n -> p (c n)"), h2T_out).then_inc(h2T_ready, 1)

        def p_third(pe, m):
            wait(pe, y_ready, m.n)
            pe.wait_ge(s2_ready, m.n + 1)
            nc.tensor.matmul(ffn_out, s2T[:, m.par, :], sW3, start=True, stop=False)
            pe.wait_ge(topwT_ready, m.n + 1)
            nc.tensor.matmul(ffn_out, topwT[:], out_bias, start=False, stop=False)
            pe.wait_ge(h2T_ready, m.n + 1)
            for c in range(KD):
                last = nc.tensor.matmul(ffn_out, h2T[:, c, :], eW3[:, c, :], start=False, stop=(c == KD - 1))
            last.then_inc(ffn_done, 1)

        def d_y(dve, m):
            dve.wait_ge(ffn_done, m.n + 1)
            wait(dve, out_stored[m.par], 16 * m.i)
            nc.vector.tensor_tensor(y[:, m.par, :], ffn_out, x2[:, m.par, :], ALU.add).then_inc(y_ready, 1)

        def supersteps(eng, slot):
            for i in range(PEEL):
                for par in range(2):
                    for g in range(GROUPS):
                        slot(Step(i, par), g)
            with eng.Fori(PEEL, T // 2) as i:
                for par in range(2):
                    for g in range(GROUPS):
                        slot(Step(i, par), g)
            for t in range(T, T + LAG + CHAIN - 1):
                for g in range(GROUPS):
                    slot(Step(t // 2, t % 2), g)

        def node(stage, eng, st, later, *more):
            m = st.back(LAG + later)
            if m.live():
                stage(eng, m, *more)

        def tiles(n):
            return min(n, T) if isinstance(n, int) else n

        def edge(stage, eng, st, g, earlier):
            s, h = before_group(st, g, earlier)
            if s.live():
                stage(eng, s, h)

        def node_work(eng, stages, edges_done=None):
            def tile_(m):
                for stage in stages:
                    if stage is d_h:
                        stage(eng, m, edges_done)
                    else:
                        stage(eng, m)
            for par in range(2):
                tile_(Step(0, par))
            with eng.Fori(1, T // 2) as i:
                for par in range(2):
                    tile_(Step(i, par))

        def all_groups(eng, body):
            for par in range(2):
                for g in range(GROUPS):
                    body(Step(0, par), g)
            with eng.Fori(1, T // 2) as i:
                for par in range(2):
                    for g in range(GROUPS):
                        body(Step(i, par), g)

        block = ctx.enter_context(nc.Block())

        @block.sync
        def _(sp):
            def load_x(m):
                wait(sp, x2_ready, m.n - 1)
                sp.dma_start(xt[:, m.par, :], x[bass.ds(m.n * P, P), :]).then_inc(x_landed[m.par], 16)

            def store(m):
                sp.wait_ge(y_ready, m.n + 1)
                sp.dma_start(out[bass.ds(m.n * P, P), :], y[:, m.par, :]).then_inc(out_stored[m.par], 16)

            for par in range(2):
                sp.dma_start(idx[:, par, :], src[par * P:(par + 1) * P, :]).then_inc(idx_landed[par], 16)
            sp.dma_start(dst_i[:].rearrange("p t k -> p (t k)"), dst).then_inc(dst_landed, 16)
            sp.dma_start(base_i[:], base).then_inc(base_landed, 16)
            sp.dma_start(wts[:], weight).then_inc(wts_landed, 16)
            sp.dma_start(wpk[:], packed).then_inc(weights_landed, 16)
            sp.dma_start(rpk[:], rows_packed).then_inc(weights_landed, 16)
            for par in range(2):
                load_x(Step(0, par))
            for par in range(2):
                load_x(Step(1, par))
            with sp.Fori(1, T // 2 - 1) as i:
                for par in range(2):
                    load_x(Step(i + 1, par))
                    store(Step(i - 1, par))
            for i in range(T // 2 - 2, T // 2):
                for par in range(2):
                    store(Step(i, par))
            for par in range(2):
                sp.wait_ge(out_stored[par], 16 * (T // 2))
                sp.wait_ge(idx_landed[par], 16 * (T // 2 + 1))

        @block.gpsimd
        def _(pool):
            nc.gpsimd.memset(ident[:], 0.0).then_inc(const_step, 1)
            pool.wait_ge(const_step, 1)
            nc.gpsimd.affine_select(out=ident[:], in_=ident[:], compare_op=ALU.not_equal, fill=1.0, base=0,
                                    pattern=[[-1, P]], channel_multiplier=1).then_inc(ident_ready, 1)
            nc.gpsimd.iota(iota_i[:], pattern=[[1, WIN]], base=0, channel_multiplier=0).then_inc(iota_ready, 1)
            nc.gpsimd.iota(lim_i[:], pattern=[[P, T], [0, GROUPS]], base=-P, channel_multiplier=0).then_inc(iota_ready, 1)
            all_groups(pool, lambda st, g: gather(pool, st, g))

        @block.scalar
        def _(act):
            nc.scalar.preload_act_table_set("natural_log_exp_and_others")
            act.wait_ge(weights_landed, 32)

            def slot(st, g):
                if g == 0:
                    wait(act, xn2T_done, tiles(st.n - 3))
                    node(a_a1, act, st, 1)
                    node(a_xn2T, act, st, 2)
                    node(a_turn, act, st, 3)
                if g == 2:
                    node(a_gex2, act, st, 2)
                edge(edge_center, act, st, g, 0)
                if g == 0:
                    node(a_inv1, act, st, 0)
                if g == 1:
                    node(a_inv2, act, st, 1)
                    node(a_first, act, st, 2)
                if g == 2:
                    node(a_s2, act, st, 2)
                    node(a_h2, act, st, 2)

            act.wait_ge(flag_ready, 1)
            with act.If(act.value_load(ordered[0:1, 0:1], min_val=0, max_val=1) != 0):
                supersteps(act, slot)
            with act.Else():
                all_groups(act, lambda st, g: edge_center(act, st, g))
                node_work(act, [a_inv1, a_a1, a_inv2, a_xn2T, a_first, a_gex2, a_s2, a_h2, a_turn])

        @block.tensor
        def _(pe):
            pe.wait_ge(ident_ready, 1)
            pe.wait_ge(bad_ready, 1)
            nc.tensor.transpose(p_D[0:1, 0:P], bad[:, 3:4], ident[:]).then_inc(bad_turned, 1)
            pe.wait_ge(weights_landed, 32)

            def slot(st, g):
                if g == 0:
                    wait(pe, y_ready, tiles(st.n - 5))
                    wait(pe, x2_ready, tiles(st.n - 3))
                    node(p_third, pe, st, 3)
                    node(p_l2, pe, st, 1)
                    node(p_first, pe, st, 2)
                if g == 1:
                    wait(pe, h2_ready, tiles(st.n - 4))
                    wait(pe, h_ready, tiles(st.n - 2))
                    node(p_xeT, pe, st, 0)
                if g == 2:
                    wait(pe, a1_ready, tiles(st.n - 2))
                    wait(pe, xn2T_ready, tiles(st.n - 3))
                    node(p_xn2T, pe, st, 1)
                edge(edge_aggregate, pe, st, g, 1)
                if g == 1:
                    node(p_second, pe, st, 2)
                if g == 2:
                    node(p_l1, pe, st, 0)
                    node(p_turn, pe, st, 2)

            def all_windows(st, g):
                J, b = st.group(g)
                with pe.Fori(0, NWIN) as win:
                    pe.wait_ge(centered, J + 1)
                    pe.wait_ge(g_sel_ready, win + (J * NWIN + 1))
                    aggregate(st, g, p_agg[0], g_agg_done)

            pe.wait_ge(flag_ready, 1)
            with pe.If(pe.value_load(ordered[0:1, 0:1], min_val=0, max_val=1) != 0):
                supersteps(pe, slot)
            with pe.Else():
                all_groups(pe, all_windows)
                node_work(pe, [p_xeT, p_l1, p_l2, p_xn2T, p_first, p_second, p_turn, p_third])

        @block.vector
        def _(dve):
            dve.wait_ge(base_landed, 16)
            dve.wait_ge(dst_landed, 16)
            dve.wait_ge(iota_ready, 2)
            base3 = base_i[:].rearrange("p (t g) -> p t g", g=GROUPS)
            for g in range(GROUPS):
                s = slice(K0[g], K0[g] + KG[g])
                nc.vector.tensor_tensor(rel[:, :, s], dst_i[:, :, s], base3[:, :, g:g + 1].to_broadcast([P, T, KG[g]]),
                                        ALU.subtract)
            nc.vector.tensor_copy(iota_f[:], iota_i[:])
            nc.vector.tensor_tensor(prog[:], base3, lim_i[:], ALU.subtract).then_inc(dve_const, 1)
            dve.wait_ge(dve_const, 1)
            nc.vector.tensor_reduce(bad[:, 0:1], rel.rearrange("p t k -> p (t k)"), AX_X, ALU.max)
            nc.vector.tensor_reduce(bad[:, 1:2], rel.rearrange("p t k -> p (t k)"), AX_X, ALU.min)
            nc.vector.tensor_reduce(bad[:, 2:3], prog[:].rearrange("p t g -> p (t g)"), AX_X, ALU.min)
            nc.vector.memset(before[:], 0.0)
            nc.vector.memset(onerow[:], 1.0)
            nc.vector.memset(topwT[:], 1.0).then_inc(dve_const, 1)
            dve.wait_ge(dve_const, 2)
            dve.wait_ge(weights_landed, 32)
            for e in range(1, NE):
                nc.vector.memset(before[:, e, 0:e], 1.0)
            e0 = COLS["eps"][0]
            nc.vector.tensor_scalar(eps1[:], wpk[:, e0:e0 + 1], 1.0, None, ALU.add)
            nc.vector.tensor_tensor(bad[:, 1:2], bad[:, 1:2], bad[:, 2:3], ALU.min).then_inc(dve_const, 1)
            dve.wait_ge(dve_const, 3)
            nc.vector.tensor_scalar(bad[:, 1:2], bad[:, 1:2], -1.0, None, ALU.mult)
            nc.vector.tensor_scalar(bad[:, 0:1], bad[:, 0:1], 1.0 - WIN, None, ALU.add).then_inc(dve_const, 1)
            dve.wait_ge(dve_const, 4)
            nc.vector.tensor_tensor(bad[:, 3:4], bad[:, 0:1], bad[:, 1:2], ALU.max).then_inc(bad_ready, 1)
            dve.wait_ge(bad_turned, 1)
            nc.vector.tensor_reduce(badmax[:], p_D[0:1, 0:P], AX_X, ALU.max).then_inc(dve_const, 1)
            dve.wait_ge(dve_const, 5)
            nc.vector.tensor_scalar(ordered[:], badmax[:], 0.0, None, ALU.is_le).then_inc(flag_ready, 1)
            nc.vector.memset(agg[:], 0.0).then_inc(agg_zeroed, 1)
            dve.wait_ge(agg_zeroed, 1)
            dve.wait_ge(wts_landed, 16)

            def slot(st, g):
                J, b = st.group(g)
                if g == 0:
                    node(d_stats1, dve, st, 0)
                if g == 1:
                    wait(dve, l2_done, tiles(st.n - 2))
                    node(d_y, dve, st, 3)
                    node(d_xe, dve, st, 0)
                    node(d_x2, dve, st, 1)
                if g == 2:
                    node(d_xn2, dve, st, 1)
                    node(d_gsoft, dve, st, 2)
                edge(edge_stats, dve, st, g, 0)
                edge(edge_finish, dve, st, g, 1)
                edge(edge_add, dve, st, g, 2)
                if g == 1:
                    node(d_gmax, dve, st, 2)
                if g == 2:
                    wait(dve, e2_done, tiles(st.n - 3))
                    adds = J - 1 if not isinstance(J, int) else min(J - 1, T * GROUPS)
                    node(d_h, dve, st, 0, lambda eng: eng.wait_ge(added, adds))
                    node(d_gtop, dve, st, 2)

            def edge_finish(eng, st, g):
                edge_scale(eng, st, g)
                edge_select(eng, st, g)

            def all_windows(st, g):
                J, b = st.group(g)
                edge_stats(dve, st, g)
                edge_scale(dve, st, g)
                K = KG[g]
                wait(dve, rel_ready, st.n + 1)
                wait(dve, g_agg_done, J * NWIN)
                gb = far_base(J)
                nc.vector.tensor_tensor(far[:, 0:K], relc[:, st.par, K0[g]:K0[g] + K], gb.to_broadcast([P, K]),
                                        ALU.add).then_inc(far_ready, 1)
                def window(win, first_node, at_end):
                    dve.wait_ge(far_ready, win + (J * NWIN + 1))
                    for k in range(K):
                        last = nc.vector.tensor_scalar(sel[:, g, k, :], iota_f[:], far[:, k:k + 1], ewr[:, g, k:k + 1],
                                                       ALU.is_equal, ALU.mult)
                    last.then_inc(g_sel_ready, 1)
                    dve.wait_ge(g_sel_ready, win + (J * NWIN + 1))
                    if not at_end:
                        nc.vector.tensor_scalar(far[:, 0:K], far[:, 0:K], float(-WIN), None, ALU.add).then_inc(far_ready, 1)
                    dve.wait_ge(g_agg_done, win + (J * NWIN + 1))
                    a = agg[:, :, bass.ds(first_node, WIN)]
                    add = nc.vector.tensor_tensor(a, p_agg[0][:, 0:KD * WIN].rearrange("p (c n) -> p c n", c=KD), a,
                                                  ALU.add)
                    if at_end:
                        add.then_inc(rows_used, 1)
                with dve.Fori(0, NWIN - 1) as win:
                    window(win, win * WIN, False)
                window(NWIN - 1, (NWIN - 1) * WIN, True)
                dve.wait_ge(rows_used, J + 1)

            def far_base(J):
                return base_i[:, bass.ds(J, 1)]

            with dve.If(dve.value_load(ordered[0:1, 0:1], min_val=0, max_val=1) != 0):
                supersteps(dve, slot)
            with dve.Else():
                all_groups(dve, all_windows)
                node_work(dve, [d_stats1, d_xe, d_h, d_x2, d_xn2, d_gmax, d_gsoft, d_gtop, d_y],
                          lambda eng: eng.wait_ge(rows_used, T * GROUPS))


def kernel(x, src, dst, edge_weight, L0_gnn_eps, L0_gnn_w1, L0_gnn_b1, L0_gnn_w2, L0_gnn_b2,
           L0_ffn_sW1, L0_ffn_sb1, L0_ffn_sW2, L0_ffn_sb2, L0_ffn_sW3, L0_ffn_sb3,
           L0_ffn_eW1, L0_ffn_eb1, L0_ffn_eW2, L0_ffn_eb2, L0_ffn_eW3, L0_ffn_eb3, L0_ffn_gW, L0_ffn_gb):
    import numpy as np
    import concourse.bacc as bacc
    from concourse.bass_utils import run_bass_kernel_spmd

    x, src, dst, edge_weight = (np.asarray(a) for a in (x, src, dst, edge_weight))
    N, E = x.shape[0], src.shape[0]
    T = -(-N // P)
    T += T % 2
    KT = -(-E // (P * T))
    KG = group_tiles(KT)

    def padded(a, n, fill):
        return np.concatenate([a, np.full((n - a.shape[0],) + a.shape[1:], fill, a.dtype)])

    def by_partition(a, fill):
        a = padded(a, T * P * KT, fill).reshape(T, P * KT)
        at, parts = 0, []
        for k in KG:
            parts.append(a[:, at:at + P * k].reshape(T, P, k))
            at += P * k
        return np.concatenate(parts, axis=2), a

    src_t, _ = by_partition(src, 0)
    dst_t, dst_flat = by_partition(dst, dst[-1])
    wts_t, _ = by_partition(edge_weight, 0)
    starts = [P * sum(KG[:g]) for g in range(GROUPS)]
    base = np.broadcast_to(dst_flat[:, starts].reshape(1, -1), (P, T * GROUPS))

    def chunks(a):
        a = np.asarray(a)
        return a.reshape(-1, P, a.shape[1]).transpose(1, 0, 2).reshape(P, -1)

    def column(a):
        return np.asarray(a).reshape(-1, P).T

    eW1 = np.asarray(L0_ffn_eW1)
    packed = np.concatenate([
        chunks(L0_gnn_w1), chunks(L0_gnn_w2), chunks(L0_ffn_sW1), chunks(L0_ffn_sW2), chunks(L0_ffn_sW3),
        eW1.reshape(NE, KD, P, EH1).transpose(2, 1, 0, 3).reshape(P, -1),
        np.asarray(L0_ffn_eW2).transpose(1, 0, 2).reshape(P, -1),
        chunks(np.asarray(L0_ffn_eW3).reshape(NE * EH2, D)), chunks(L0_ffn_gW),
        column(L0_gnn_b1), column(L0_ffn_sb1), column(L0_ffn_sb2), column(L0_ffn_eb1),
        np.broadcast_to(np.asarray(L0_gnn_eps).reshape(1, 1), (P, 1))], axis=1)
    biases = np.concatenate([np.asarray(a).reshape(1, -1) for a in (L0_gnn_b2, L0_ffn_eb2, L0_ffn_gb)], axis=1)
    rows_packed = np.concatenate([
        np.concatenate([np.asarray(L0_ffn_eb3), np.asarray(L0_ffn_sb3).reshape(1, -1)]),
        padded(biases, NE + 1, 0)], axis=1)

    arrays = {"x": padded(x, T * P, 0), "src": padded(src_t.reshape(T * P, KT), (T + 2) * P, 0),
              "dst": dst_t.transpose(1, 0, 2).reshape(P, T * KT),
              "weight": wts_t.transpose(1, 0, 2).reshape(P, T * KT),
              "base": base, "packed": packed, "rows_packed": rows_packed}
    arrays = {f"in_{n}": np.ascontiguousarray(a) for n, a in arrays.items()}
    nc = bacc.Bacc("TRN2", target_bir_lowering=False, num_devices=1)
    args = [nc.dram_tensor(n, a.shape, mybir.dt.from_np(a.dtype), kind="ExternalInput").ap() for n, a in arrays.items()]
    out = nc.dram_tensor("out", (T * P, D), F32, kind="ExternalOutput").ap()
    build(nc, *args, out)
    r = run_bass_kernel_spmd(nc, [arrays], core_ids=[0])
    return r.results[0]["out"][:N]
```

```python
from contextlib import ExitStack

import concourse.bass as bass
from concourse import mybir

ALU = mybir.AluOpType
ACT = mybir.ActivationFunctionType
F32 = mybir.dt.float32
I32 = mybir.dt.int32
AX_X = mybir.AxisListType.X

P = 128
D = 256
KD = D // P
WIN = 64
GROUPS = 3
NE = 4
EH1, EH2 = 128, 64
SH2 = 128
TOPK = 2
LN_EPS = 1e-5
LAG = 2
CHAIN = 5
PEEL = 3
AHEAD = 2
MAX_CHUNK = 8


def group_tiles(tiles):
    return [(tiles + GROUPS - 1 - g) // GROUPS for g in range(GROUPS)]


def weight_columns():
    at, out = 0, {}
    for name, width in (("w1", KD * D), ("w2", KD * D), ("sW1", KD * D), ("sW2", KD * SH2), ("sW3", D),
                        ("eW1", KD * NE * EH1), ("eW2", NE * EH2), ("eW3", KD * D), ("gW", KD * NE),
                        ("b1", KD), ("sb1", KD), ("sb2", 1), ("eb1", NE), ("eps", 1)):
        out[name] = (at, width)
        at += width
    return out, at


def build(nc, x, src, dst, weight, base, packed, rows_packed, xn, out):
    T = x.shape[0] // P
    KT = src.shape[1] // (T + AHEAD)
    KG = group_tiles(KT)
    K0 = [sum(KG[:g]) for g in range(GROUPS)]
    KMAX = max(KG)
    NPAD = T * P + WIN
    NWIN = T * P // WIN
    COLS, WCOLS = weight_columns()
    assert T % 2 == 0 and T // 2 > PEEL
    R = max(r for r in range(1, MAX_CHUNK + 1) if T // 2 % r == 0 and r < T // 2)
    CHUNKS = T // R

    with ExitStack() as ctx:
        def sb(name, shape, dt=F32):
            return ctx.enter_context(nc.sbuf_tensor(name, shape, dt))

        def bank(name):
            return ctx.enter_context(nc.psum_tensor(name, [P, 512], F32))

        def sem(name):
            return ctx.enter_context(nc.semaphore(name))

        agg = sb("agg", [P, KD, NPAD])
        xs = agg[:].rearrange("p k n -> p (k n)")[:, 0:T * D].rearrange("p (r d) -> p r d", d=D)
        src_i = sb("src_i", [P, (T + AHEAD) * KT], I32)
        idx = sb("idx", [P, 2, KT], I32)
        rows = sb("rows", [P, 2, KT, D])
        dst_i = sb("dst_i", [P, T + AHEAD, KT], I32)
        rel = dst_i[:].bitcast(F32)
        wts = sb("wts", [P, (T + AHEAD) * KT])
        base_i = sb("base_i", [P, T * GROUPS], I32)
        prog = sb("prog", [P, T, GROUPS])
        relc = sb("relc", [P, KT])
        wc = sb("wc", [P, KT])
        sel = sb("sel", [P, GROUPS, KMAX, WIN])
        cst6 = sb("cst6", [P, R, 6])
        cwork = sb("cwork", [P, R, 5])
        cnmean = sb("cnmean", [P, R])
        cvar = sb("cvar", [P, R])
        clog = sb("clog", [P, R])
        cinv0 = sb("cinv0", [P, R])
        cnewt = sb("cnewt", [P, 2, R])
        cinv = sb("cinv", [P, R])
        cbias = sb("cbias", [P, R])
        wpk = sb("wpk", [P, WCOLS])
        rpk = sb("rpk", [NE + 1, 3 * D + NE])
        xt = sb("xt", [P, 2, D])
        xnt = sb("xnt", [P, 2, D])
        y = sb("y", [P, 2, D])
        hT = sb("hT", [P, KD, P])
        a1T = sb("a1T", [P, KD, P])
        xn2 = sb("xn2", [P, D])
        xn2T = sb("xn2T", [P, KD, P])
        s1T = sb("s1T", [P, KD, P])
        s2T = sb("s2T", [P, 2, P])
        e1T = sb("e1T", [P, NE, P])
        h2 = sb("h2", [P, D])
        h2T = sb("h2T", [P, KD, P])
        topwT = sb("topwT", [NE + 1, P])
        st6 = sb("st6", [P, 1, 6])
        nwork = sb("nwork", [P, 1, 5])
        nmean = sb("nmean", [P, 2])
        var = sb("var", [P, 2])
        lnv = sb("lnv", [P, 1])
        inv0 = sb("inv0", [P, 2])
        newt = sb("newt", [P, 2])
        inv = sb("inv", [P, 1])
        gmax = sb("gmax", [P, 2])
        gex = sb("gex", [P, NE])
        gsum = sb("gsum", [P, 5])
        gp = sb("gp", [P, NE])
        gex2 = sb("gex2", [P, NE])
        gcmp = sb("gcmp", [P, 3, NE, NE])
        grank = sb("grank", [P, NE])
        gkeep = sb("gkeep", [P, NE])
        topw = sb("topw", [P, NE])
        ident = sb("ident", [P, P])
        onerow = sb("onerow", [1, P])
        eps1 = sb("eps1", [P, 1])
        iota_i = sb("iota_i", [P, WIN], I32)
        iota_f = sb("iota_f", [P, WIN])
        lim_i = sb("lim_i", [P, T, GROUPS], I32)
        before = sb("before", [P, NE, NE])
        bad = sb("bad", [P, 4])
        badmax = sb("badmax", [1, 1])
        ordered = sb("ordered", [1, 1], I32)
        far = sb("far", [P, KMAX])

        p_agg = [bank(f"p_agg{n}") for n in range(2)]
        p_A = bank("p_A")
        p_B = bank("p_B")
        p_C = bank("p_C")
        p_D = bank("p_D")
        p_E = bank("p_E")
        p_F = bank("p_F")
        l2_out, ffn_out = p_A[:, 0:D], p_A[:, D:2 * D]
        s1_out, logits = p_B[:, 0:D], p_B[:, D:D + NE]
        xnT_out, h2T_out = p_D[:, 0:D], p_D[:, D:2 * D]
        e2_out, s2_out, topwT_out = p_E[:, 0:D], p_E[:, D:D + SH2], p_E[0:NE, D + SH2:D + SH2 + P]
        l1_out, xn2T_out = p_F[:, 0:D], p_F[:, D:2 * D]

        def w(name, *dims):
            a, n = COLS[name]
            v = wpk[:, a:a + n]
            return v.rearrange("p (k n) -> p k n", k=dims[0]) if dims else v

        w1, w2, sW1, eW3 = (w(n, KD) for n in ("w1", "w2", "sW1", "eW3"))
        sW2, gW = w("sW2", KD), w("gW", KD)
        sW3 = w("sW3")
        eW1 = w("eW1", KD * NE)
        eW2 = w("eW2", NE)
        out_bias = rpk[:, 0:D]
        b2_row, eb2_row, gb_row = rpk[0:1, D:2 * D], rpk[0:1, 2 * D:3 * D], rpk[0:1, 3 * D:3 * D + NE]

        rows_landed = [sem(f"rows_landed{n}") for n in range(2 * GROUPS)]
        chunk_landed = [sem(f"chunk_landed{n}") for n in range(2)]
        xn_stored = sem("xn_stored")
        x_landed = [sem(f"x_landed{n}") for n in range(2)]
        xn_landed = [sem(f"xn_landed{n}") for n in range(2)]
        out_stored = [sem(f"out_stored{n}") for n in range(2)]
        src_landed, dst_landed, base_landed = sem("src_landed"), sem("dst_landed"), sem("base_landed")
        weights_landed, wts_landed = sem("weights_landed"), sem("wts_landed")
        rows_turn = sem("rows_turn")
        const_step, ident_ready, iota_ready = sem("const_step"), sem("ident_ready"), sem("iota_ready")
        bad_ready, bad_turned, flag_ready = sem("bad_ready"), sem("bad_turned"), sem("flag_ready")
        dve_const, agg_zeroed = sem("dve_const"), sem("agg_zeroed")
        c_bn, c_mv, c_stats, c_log, c_inv0 = (sem(s) for s in ("c_bn", "c_mv", "c_stats", "c_log", "c_inv0"))
        c_newton = sem("c_newton")
        normed, stats_turn = sem("normed"), sem("stats_turn")
        idx_ready, rel_ready = sem("idx_ready"), sem("rel_ready")
        sel_ready, rows_used, added = sem("sel_ready"), sem("rows_used"), sem("added")
        far_ready, g_sel_ready, g_agg_done = sem("far_ready"), sem("g_sel_ready"), sem("g_agg_done")
        n_bn, n_mv, n_stats, n_log, n_inv0 = (sem(s) for s in ("n_bn", "n_mv", "n_stats", "n_log", "n_inv0"))
        n_newton = sem("n_newton")
        xnT_done, h_ready, l1_done, a1_ready = (sem(s) for s in ("xnT_done", "h_ready", "l1_done", "a1_ready"))
        l2_done, x2_ready, xn2_ready, xn2T_done, xn2T_ready = (sem(s) for s in ("l2_done", "x2_ready", "xn2_ready", "xn2T_done", "xn2T_ready"))
        s1_done, e1_done = sem("s1_done"), sem("e1_done")
        gmax_step, gex_ready, gsoft_step = sem("gmax_step"), sem("gex_ready"), sem("gsoft_step")
        gex2_ready, gtop_step = sem("gex2_ready"), sem("gtop_step")
        s1_ready, e1_ready, s2_done, e2_done, s2_ready = (sem(s) for s in ("s1_ready", "e1_ready", "s2_done", "e2_done", "s2_ready"))
        h2_ready, h2T_done, topwT_done, h2T_ready, topwT_ready = (sem(s) for s in ("h2_ready", "h2T_done", "topwT_done", "h2T_ready", "topwT_ready"))
        ffn_done, y_ready = sem("ffn_done"), sem("y_ready")
        GSOFT, GTOP = 9, 4

        def wait(eng, s, value):
            if not isinstance(value, int) or value > 0:
                eng.wait_ge(s, value)

        class Step:

            def __init__(self, i, par):
                self.i, self.par = (i + par // 2, par % 2) if par // 2 else (i, par % 2)
                self.n = self.i * 2 + self.par

            def back(self, k):
                return Step(self.i, self.par - k)

            def live(self):
                return not isinstance(self.i, int) or 0 <= self.n < T

            def group(self, g):
                return self.n * GROUPS + g, self.par * GROUPS + g

        def before_group(st, g, k):
            j = g - k
            return (st.back(-(j // GROUPS)), j % GROUPS)

        def gather(pool, st, g):
            J, b = st.group(g)
            wait(pool, idx_ready, J + 1)
            wait(pool, rows_used, J - 2 * GROUPS + 1)
            pool.sem_inc(rows_turn, 1)
            for k in range(K0[g], K0[g] + KG[g]):
                nc.gpsimd.indirect_dma_start(
                    rows[:, st.par, k, :], None, xn,
                    bass.IndirectOffsetOnAxis(idx[:, st.par, k:k + 1], 0)).then_inc(rows_landed[b], 16)

        def moments(dve, st6_, work, nmean, v, steps, first):
            K = st6_.shape[1]
            halves = st6_.rearrange("p k (h s) -> p k h s", h=2)
            total, lead, square, spread = work[:, 0:K, 0:2], work[:, 0:K, 2], work[:, 0:K, 3], work[:, 0:K, 4]
            nc.vector.tensor_tensor(total, halves[:, :, 0, 1:3], halves[:, :, 1, 1:3], ALU.add)
            nc.vector.tensor_tensor(lead, halves[:, :, 0, 1], halves[:, :, 1, 1], ALU.subtract).then_inc(steps, 1)
            dve.wait_ge(steps, first + 1)
            nc.vector.tensor_scalar(nmean, total[:, :, 0], -0.5, None, ALU.mult)
            nc.vector.scalar_tensor_tensor(out=square, in0=lead, scalar=0.25, in1=lead, op0=ALU.mult, op1=ALU.mult)
            nc.vector.tensor_scalar(spread, total[:, :, 1], 1.0 / D, LN_EPS, ALU.mult, ALU.add).then_inc(steps, 1)
            dve.wait_ge(steps, first + 2)
            return nc.vector.tensor_tensor(v, square, spread, ALU.add)

        def newton(dve, v, y0, new, inv_, steps, first):
            nc.vector.scalar_tensor_tensor(out=new[0], in0=y0, scalar=-0.5, in1=y0,
                                           op0=ALU.mult, op1=ALU.mult).then_inc(steps, 1)
            dve.wait_ge(steps, first + 1)
            nc.vector.tensor_tensor(new[1], new[0], v, ALU.mult).then_inc(steps, 1)
            dve.wait_ge(steps, first + 2)
            nc.vector.scalar_tensor_tensor(out=inv_, in0=new[1], scalar=1.5, in1=y0,
                                           op0=ALU.add, op1=ALU.mult).then_inc(steps, 1)
            dve.wait_ge(steps, first + 3)

        def chunk_rows(c):
            return bass.ds(c.n * R, R)

        def chunk_stats(dve, c):
            dve.wait_ge(chunk_landed[c.par], 16 * (c.i + 1))
            dve.sem_inc(stats_turn, 1)
            for r in range(R):
                last = nc.vector.bn_stats(cst6[:, r, :], xs[:, bass.ds(c.n * R + r, 1), :].rearrange("p r d -> p (r d)"))
            last.then_inc(c_bn, 1)
            dve.wait_ge(c_bn, c.n + 1)
            moments(dve, cst6[:], cwork, cnmean[:], cvar[:], c_mv, 2 * c.n).then_inc(c_stats, 1)
            dve.wait_ge(c_inv0, c.n + 1)
            newton(dve, cvar[:], cinv0[:], (cnewt[:, 0, :], cnewt[:, 1, :]), cinv[:],
                   c_newton, 4 * c.n)
            nc.vector.tensor_tensor(cbias[:], cnmean[:], cinv[:], ALU.mult
                                    ).then_inc(c_newton, 1)

        def chunk_norm(act, c):
            act.wait_ge(c_stats, c.n + 1)
            nc.scalar.activation(clog[:], cvar[:], ACT.Ln).then_inc(c_log, 1)
            act.wait_ge(c_log, c.n + 1)
            nc.scalar.activation(cinv0[:], clog[:], ACT.Exp, scale=-0.5).then_inc(c_inv0, 1)
            act.wait_ge(c_newton, 4 * c.n + 4)
            for r in range(R):
                row = xs[:, bass.ds(c.n * R + r, 1), :].rearrange("p r d -> p (r d)")
                last = nc.scalar.activation(row, row, ACT.Identity, bias=cbias[:, r:r + 1],
                                            scale=cinv[:, r:r + 1])
            last.then_inc(normed, 1)
            act.wait_ge(normed, c.n + 1)
            nc.scalar.dma_start(xn.rearrange("(p r) d -> p r d", p=P)[:, chunk_rows(c), :], xs[:, chunk_rows(c), :]
                                ).then_inc(xn_stored, 16)

        def all_chunks(eng, stage):
            with eng.Fori(0, CHUNKS // 2) as i:
                for par in range(2):
                    stage(eng, Step(i, par))

        def copy_sources(dve, st, g):
            nc.vector.tensor_copy(idx[:, st.par, K0[g]:K0[g] + KG[g]], src_i[:, bass.ds(st.n * KT + K0[g], KG[g])]
                                  ).then_inc(idx_ready, 1)

        def sources_ahead(dve, st, g):
            J, b = st.group(g)
            wait(dve, rows_used, J)
            copy_sources(dve, *before_group(st, g, 1 - 2 * GROUPS))

        def copy_edges(dve, st):
            at = bass.ds(st.n * KT, KT)
            nc.vector.tensor_copy(wc[:], wts[:, at])
            nc.vector.tensor_copy(relc[:], rel.rearrange("p t k -> p (t k)")[:, at]).then_inc(rel_ready, 1)

        def edge_select(dve, st, g):
            J, b = st.group(g)
            if g == 0:
                wait(dve, sel_ready, J)
                copy_edges(dve, st)
            wait(dve, rel_ready, st.n + 1)
            wait(dve, rows_used, J - GROUPS + 1)
            for k in range(K0[g], K0[g] + KG[g]):
                last = nc.vector.tensor_scalar(sel[:, g, k - K0[g], :], iota_f[:], relc[:, k:k + 1], wc[:, k:k + 1],
                                               ALU.is_equal, ALU.mult)
            last.then_inc(sel_ready, 1)

        def aggregate(st, g, bank_, done):
            for c in range(KD):
                for k in range(KG[g]):
                    last = nc.tensor.matmul(bank_[:, c * WIN:(c + 1) * WIN],
                                            rows[:, st.par, K0[g] + k, c * P:(c + 1) * P], sel[:, g, k, :],
                                            start=(k == 0), stop=(k == KG[g] - 1))
            last.then_inc(done, 1)

        def edge_aggregate(pe, st, g):
            J, b = st.group(g)
            pe.wait_ge(sel_ready, J + 1)
            pe.wait_ge(rows_landed[b], 16 * KG[g] * (st.i + 1))
            wait(pe, added, J - 1)
            aggregate(st, g, p_agg[b % 2], rows_used)

        def edge_add(dve, st, g):
            J, b = st.group(g)
            at = dve.value_load(base_i[0:1, bass.ds(J, 1)], min_val=0, max_val=T * P)
            dve.wait_ge(rows_used, J + 1)
            wait(dve, added, J)
            a = agg[:, :, bass.ds(at, WIN)]
            nc.vector.tensor_tensor(a, p_agg[b % 2][:, 0:KD * WIN].rearrange("p (c n) -> p c n", c=KD), a,
                                    ALU.add).then_inc(added, 1)

        def p_xnT(pe, m):
            pe.wait_ge(xn_landed[m.par], 16 * (m.i + 1))
            wait(pe, h_ready, m.n)
            for c in range(KD):
                last = nc.tensor.transpose(xnT_out[:, c * P:(c + 1) * P], xnt[:, m.par, c * P:(c + 1) * P], ident[:])
            last.then_inc(xnT_done, 1)

        def d_h(dve, m, edges_done):
            dve.wait_ge(xnT_done, m.n + 1)
            edges_done(dve)
            wait(dve, l1_done, m.n)
            nc.vector.scalar_tensor_tensor(out=hT[:], in0=xnT_out.rearrange("p (c n) -> p c n", c=KD), scalar=eps1[:],
                                           in1=tile_of(agg, m), op0=ALU.mult, op1=ALU.add).then_inc(h_ready, 1)

        def tile_of(a, m):
            return a[:, :, bass.ds(m.n * P, P)]

        def p_l1(pe, m):
            pe.wait_ge(h_ready, m.n + 1)
            wait(pe, a1_ready, m.n)
            for o in range(KD):
                for c in range(KD):
                    last = nc.tensor.matmul(l1_out[:, o * P:(o + 1) * P], w1[:, c, o * P:(o + 1) * P], hT[:, c, :],
                                            start=(c == 0), stop=(c == KD - 1))
            last.then_inc(l1_done, 1)

        def a_a1(act, m):
            act.wait_ge(l1_done, m.n + 1)
            wait(act, l2_done, m.n)
            b = COLS["b1"][0]
            for o in range(KD):
                last = nc.scalar.activation(a1T[:, o, :], l1_out[:, o * P:(o + 1) * P], ACT.Relu,
                                            bias=wpk[:, b + o:b + o + 1])
            last.then_inc(a1_ready, 1)

        def p_l2(pe, m):
            pe.wait_ge(a1_ready, m.n + 1)
            wait(pe, x2_ready, m.n)
            for c in range(KD):
                nc.tensor.matmul(l2_out, a1T[:, c, :], w2[:, c, :], start=(c == 0), stop=False)
            nc.tensor.matmul(l2_out, onerow[:], b2_row, start=False, stop=True).then_inc(l2_done, 1)

        def d_x2(dve, m):
            dve.wait_ge(l2_done, m.n + 1)
            dve.wait_ge(x_landed[m.par], 16 * (m.i + 1))
            dve.wait_ge(h_ready, m.n + 1)
            nc.vector.tensor_tensor(tile_of(agg, m), l2_out.rearrange("p (c n) -> p c n", c=KD),
                                    xt[:, m.par, :].rearrange("p (c n) -> p c n", c=KD), ALU.add).then_inc(x2_ready, 1)
            dve.wait_ge(x2_ready, m.n + 1)
            dve.sem_inc(stats_turn, 1)
            nc.vector.bn_stats(st6[:, 0, :], tile_of(agg, m)).then_inc(n_bn, 1)
            dve.wait_ge(n_bn, m.n + 1)
            moments(dve, st6[:], nwork, nmean[:, m.par:m.par + 1], var[:, m.par:m.par + 1], n_mv, 2 * m.n
                    ).then_inc(n_stats, 1)

        def a_inv2(act, m):
            act.wait_ge(n_stats, m.n + 1)
            wait(act, n_inv0, m.n)
            nc.scalar.activation(lnv[:], var[:, m.par:m.par + 1], ACT.Ln).then_inc(n_log, 1)
            act.wait_ge(n_log, m.n + 1)
            nc.scalar.activation(inv0[:, m.par:m.par + 1], lnv[:], ACT.Exp, scale=-0.5).then_inc(n_inv0, 1)

        def d_xn2(dve, m):
            dve.wait_ge(n_inv0, m.n + 1)
            newton(dve, var[:, m.par:m.par + 1], inv0[:, m.par:m.par + 1], (newt[:, 0:1], newt[:, 1:2]), inv[:],
                   n_newton, 3 * m.n)
            wait(dve, xn2T_done, m.n)
            nc.vector.tensor_scalar(xn2[:].rearrange("p (c n) -> p c n", c=KD), tile_of(agg, m),
                                    nmean[:, m.par:m.par + 1], inv[:], ALU.add, ALU.mult).then_inc(xn2_ready, 1)

        def p_xn2T(pe, m):
            pe.wait_ge(xn2_ready, m.n + 1)
            wait(pe, xn2T_ready, m.n)
            for c in range(KD):
                last = nc.tensor.transpose(xn2T_out[:, c * P:(c + 1) * P], xn2[:, c * P:(c + 1) * P], ident[:])
            last.then_inc(xn2T_done, 1)

        def a_xn2T(act, m):
            act.wait_ge(xn2T_done, m.n + 1)
            wait(act, e1_done, m.n)
            nc.scalar.copy(xn2T[:].rearrange("p c n -> p (c n)"), xn2T_out).then_inc(xn2T_ready, 1)

        def p_first(pe, m):
            pe.wait_ge(xn2T_ready, m.n + 1)
            wait(pe, s1_ready, m.n)
            for c in range(KD):
                nc.tensor.matmul(logits, xn2T[:, c, :], gW[:, c, :], start=(c == 0), stop=False)
            nc.tensor.matmul(logits, onerow[:], gb_row, start=False, stop=True)
            for o in range(KD):
                for c in range(KD):
                    last = nc.tensor.matmul(s1_out[:, o * P:(o + 1) * P], sW1[:, c, o * P:(o + 1) * P], xn2T[:, c, :],
                                            start=(c == 0), stop=(c == KD - 1))
            last.then_inc(s1_done, 1)
            wait(pe, e1_ready, m.n)
            for e in range(NE):
                for c in range(KD):
                    last = nc.tensor.matmul(p_C[:, e * P:(e + 1) * P], eW1[:, c * NE + e, :], xn2T[:, c, :],
                                            start=(c == 0), stop=(c == KD - 1))
            last.then_inc(e1_done, 1)

        def d_gmax(dve, m):
            dve.wait_ge(s1_done, m.n + 1)
            nc.vector.tensor_reduce(gmax[:, 0:1], logits, AX_X, ALU.max).then_inc(gmax_step, 1)
            dve.wait_ge(gmax_step, 2 * m.n + 1)
            nc.vector.tensor_scalar(gmax[:, 1:2], gmax[:, 0:1], -1.0, None, ALU.mult).then_inc(gmax_step, 1)

        def a_first(act, m):
            act.wait_ge(gmax_step, 2 * m.n + 2)
            nc.scalar.activation(gex[:], logits, ACT.Exp, bias=gmax[:, 1:2]).then_inc(gex_ready, 1)
            act.wait_ge(s1_done, m.n + 1)
            wait(act, s2_done, m.n)
            b = COLS["sb1"][0]
            for o in range(KD):
                last = nc.scalar.activation(s1T[:, o, :], s1_out[:, o * P:(o + 1) * P], ACT.Relu,
                                            bias=wpk[:, b + o:b + o + 1])
            last.then_inc(s1_ready, 1)
            act.wait_ge(e1_done, m.n + 1)
            wait(act, e2_done, m.n)
            b = COLS["eb1"][0]
            for e in range(NE):
                last = nc.scalar.activation(e1T[:, e, :], p_C[:, e * P:(e + 1) * P], ACT.Relu,
                                            bias=wpk[:, b + e:b + e + 1])
            last.then_inc(e1_ready, 1)

        def p_second(pe, m):
            pe.wait_ge(s1_ready, m.n + 1)
            wait(pe, topwT_ready, m.n)
            for c in range(KD):
                last = nc.tensor.matmul(s2_out, sW2[:, c, :], s1T[:, c, :], start=(c == 0), stop=(c == KD - 1))
            last.then_inc(s2_done, 1)
            pe.wait_ge(e1_ready, m.n + 1)
            for e in range(NE):
                o = e2_out[:, e * EH2:(e + 1) * EH2]
                nc.tensor.matmul(o, e1T[:, e, :], eW2[:, e, :], start=True, stop=False)
                last = nc.tensor.matmul(o, onerow[:], eb2_row[:, e * EH2:(e + 1) * EH2], start=False, stop=True)
            last.then_inc(e2_done, 1)

        def a_s2(act, m):
            act.wait_ge(e2_done, m.n + 1)
            wait(act, ffn_done, m.n - 1)
            b = COLS["sb2"][0]
            nc.scalar.activation(s2T[:, m.par, :], s2_out, ACT.Relu, bias=wpk[:, b:b + 1]).then_inc(s2_ready, 1)

        def d_gsoft(dve, m):
            n = [GSOFT * m.n]
            by_row = gp[:].unsqueeze(1).to_broadcast([P, NE, NE])
            by_col = gp[:].unsqueeze(2).to_broadcast([P, NE, NE])

            def step(ins, after=True):
                ins.then_inc(gsoft_step, 1)
                n[0] = n[0] + 1
                dve.wait_ge(gsoft_step, n[0])

            dve.wait_ge(gex_ready, m.n + 1)
            step(nc.vector.reduce_sum(gsum[:, 0:1], gex[:], AX_X))
            step(nc.vector.reciprocal(gsum[:, 1:2], gsum[:, 0:1]))
            step(nc.vector.tensor_scalar(gp[:], gex[:], gsum[:, 1:2], None, ALU.mult))
            step(nc.vector.tensor_scalar(gsum[:, 2:3], gsum[:, 1:2], -1.0, None, ALU.mult))
            step(nc.vector.tensor_tensor(gcmp[:, 0], by_row, by_col, ALU.is_gt))
            step(nc.vector.tensor_tensor(gcmp[:, 1], by_row, by_col, ALU.is_equal))
            step(nc.vector.tensor_tensor(gcmp[:, 2], gcmp[:, 1], before[:], ALU.mult))
            step(nc.vector.tensor_tensor(gcmp[:, 1], gcmp[:, 2], gcmp[:, 0], ALU.add))
            step(nc.vector.tensor_reduce(grank[:], gcmp[:, 1], AX_X, ALU.add))

        def a_gex2(act, m):
            act.wait_ge(gsoft_step, GSOFT * m.n + 4)
            wait(act, gtop_step, GTOP * m.n)
            nc.scalar.activation(gex2[:], gp[:], ACT.Exp, bias=gsum[:, 2:3]).then_inc(gex2_ready, 1)

        def d_gtop(dve, m):
            dve.wait_ge(gex2_ready, m.n + 1)
            wait(dve, topwT_done, m.n)
            n = GTOP * m.n
            nc.vector.scalar_tensor_tensor(out=gkeep[:], in0=grank[:], scalar=TOPK - 0.5, in1=gex2[:],
                                           op0=ALU.is_lt, op1=ALU.mult).then_inc(gtop_step, 1)
            dve.wait_ge(gtop_step, n + 1)
            nc.vector.reduce_sum(gsum[:, 3:4], gkeep[:], AX_X).then_inc(gtop_step, 1)
            dve.wait_ge(gtop_step, n + 2)
            nc.vector.reciprocal(gsum[:, 4:5], gsum[:, 3:4]).then_inc(gtop_step, 1)
            dve.wait_ge(gtop_step, n + 3)
            nc.vector.tensor_scalar(topw[:], gkeep[:], gsum[:, 4:5], None, ALU.mult).then_inc(gtop_step, 1)

        def a_h2(act, m):
            act.wait_ge(e2_done, m.n + 1)
            act.wait_ge(gtop_step, GTOP * m.n + GTOP)
            wait(act, h2T_done, m.n)
            for e in range(NE):
                s = slice(e * EH2, (e + 1) * EH2)
                last = nc.scalar.activation(h2[:, s], e2_out[:, s], ACT.Relu, scale=topw[:, e:e + 1])
            last.then_inc(h2_ready, 1)

        def p_topwT(pe, m):
            pe.wait_ge(gtop_step, GTOP * m.n + GTOP)
            pe.wait_ge(s2_ready, m.n + 1)
            pe.wait_ge(h2_ready, m.n + 1)
            nc.tensor.transpose(topwT_out, topw[:], ident[:]).then_inc(topwT_done, 1)

        def p_h2T(pe, m):
            pe.wait_ge(h2_ready, m.n + 1)
            wait(pe, h2T_ready, m.n)
            for c in range(KD):
                last = nc.tensor.transpose(h2T_out[:, c * P:(c + 1) * P], h2[:, c * P:(c + 1) * P], ident[:])
            last.then_inc(h2T_done, 1)

        def a_topwT(act, m):
            act.wait_ge(topwT_done, m.n + 1)
            wait(act, ffn_done, m.n)
            if isinstance(m.n, int) and m.n == 0:
                act.wait_ge(dve_const, 3)
            nc.scalar.copy(topwT[0:NE, :], topwT_out).then_inc(topwT_ready, 1)

        def a_h2T(act, m):
            act.wait_ge(h2T_done, m.n + 1)
            wait(act, ffn_done, m.n)
            nc.scalar.copy(h2T[:].rearrange("p c n -> p (c n)"), h2T_out).then_inc(h2T_ready, 1)

        def p_third(pe, m):
            wait(pe, y_ready, m.n)
            pe.wait_ge(s2_ready, m.n + 1)
            nc.tensor.matmul(ffn_out, s2T[:, m.par, :], sW3, start=True, stop=False)
            pe.wait_ge(topwT_ready, m.n + 1)
            nc.tensor.matmul(ffn_out, topwT[:], out_bias, start=False, stop=False)
            pe.wait_ge(h2T_ready, m.n + 1)
            for c in range(KD):
                last = nc.tensor.matmul(ffn_out, h2T[:, c, :], eW3[:, c, :], start=False, stop=(c == KD - 1))
            last.then_inc(ffn_done, 1)

        def d_y(dve, m):
            dve.wait_ge(ffn_done, m.n + 1)
            wait(dve, out_stored[m.par], 16 * m.i)
            nc.vector.tensor_tensor(y[:, m.par, :].rearrange("p (c n) -> p c n", c=KD),
                                    ffn_out.rearrange("p (c n) -> p c n", c=KD), tile_of(agg, m), ALU.add
                                    ).then_inc(y_ready, 1)

        def supersteps(eng, slot):
            for i in range(PEEL):
                for par in range(2):
                    for g in range(GROUPS):
                        slot(Step(i, par), g)
            with eng.Fori(PEEL, T // 2) as i:
                for par in range(2):
                    for g in range(GROUPS):
                        slot(Step(i, par), g)
            for t in range(T, T + LAG + CHAIN - 1):
                for g in range(GROUPS):
                    slot(Step(t // 2, t % 2), g)

        def node(stage, eng, st, later, *more):
            m = st.back(LAG + later)
            if m.live():
                stage(eng, m, *more)

        def tiles(n):
            return min(n, T) if isinstance(n, int) else n

        def edge(stage, eng, st, g, earlier):
            s, h = before_group(st, g, earlier)
            if s.live():
                stage(eng, s, h)

        def node_work(eng, stages, edges_done=None):
            def tile_(m):
                for stage in stages:
                    if stage is d_h:
                        stage(eng, m, edges_done)
                    else:
                        stage(eng, m)
            for par in range(2):
                tile_(Step(0, par))
            with eng.Fori(1, T // 2) as i:
                for par in range(2):
                    tile_(Step(i, par))

        def all_groups(eng, body):
            for par in range(2):
                for g in range(GROUPS):
                    body(Step(0, par), g)
            with eng.Fori(1, T // 2) as i:
                for par in range(2):
                    for g in range(GROUPS):
                        body(Step(i, par), g)

        block = ctx.enter_context(nc.Block())

        @block.sync
        def _(sp):
            def load_chunk(c):
                wait(sp, chunk_landed[c.par], 16 * c.i)
                sp.dma_start(xs[:, chunk_rows(c), :], x.rearrange("(p r) d -> p r d", p=P)[:, chunk_rows(c), :]
                             ).then_inc(chunk_landed[c.par], 16)

            def load_xn(m):
                wait(sp, xnT_done, m.n - 1)
                sp.dma_start(xnt[:, m.par, :], xn[bass.ds(m.n * P, P), :]).then_inc(xn_landed[m.par], 16)

            def load_x(m):
                wait(sp, x2_ready, m.n - 1)
                sp.dma_start(xt[:, m.par, :], x[bass.ds(m.n * P, P), :]).then_inc(x_landed[m.par], 16)

            def store(m):
                sp.wait_ge(y_ready, m.n + 1)
                sp.dma_start(out[bass.ds(m.n * P, P), :], y[:, m.par, :]).then_inc(out_stored[m.par], 16)

            for par in range(2):
                load_chunk(Step(0, par))
            with sp.Fori(1, CHUNKS // 2) as i:
                for par in range(2):
                    load_chunk(Step(i, par))
            sp.dma_start(dst_i[:].rearrange("p t k -> p (t k)"), dst).then_inc(dst_landed, 16)
            sp.dma_start(base_i[:], base).then_inc(base_landed, 16)
            sp.dma_start(src_i[:], src).then_inc(src_landed, 16)
            sp.dma_start(wts[:], weight).then_inc(wts_landed, 16)
            sp.dma_start(wpk[:], packed).then_inc(weights_landed, 16)
            sp.dma_start(rpk[:], rows_packed).then_inc(weights_landed, 16)
            sp.wait_ge(xn_stored, 16 * CHUNKS)

            def serve(m, first=False):
                load_xn(m)
                if not first:
                    load_x(m.back(1))

            serve(Step(0, 0), True)
            for m in range(1, 4):
                serve(Step(m // 2, m % 2))
            with sp.Fori(2, T // 2) as i:
                for par in range(2):
                    serve(Step(i, par))
                    store(Step(i - 2, par))
            load_x(Step(T // 2 - 1, 1))
            for i in range(T // 2 - 2, T // 2):
                for par in range(2):
                    store(Step(i, par))
            for par in range(2):
                sp.wait_ge(out_stored[par], 16 * (T // 2))

        @block.gpsimd
        def _(pool):
            nc.gpsimd.memset(ident[:], 0.0).then_inc(const_step, 1)
            pool.wait_ge(const_step, 1)
            nc.gpsimd.affine_select(out=ident[:], in_=ident[:], compare_op=ALU.not_equal, fill=1.0, base=0,
                                    pattern=[[-1, P]], channel_multiplier=1).then_inc(ident_ready, 1)
            nc.gpsimd.iota(iota_i[:], pattern=[[1, WIN]], base=0, channel_multiplier=0).then_inc(iota_ready, 1)
            nc.gpsimd.iota(lim_i[:], pattern=[[P, T], [0, GROUPS]], base=-P, channel_multiplier=0).then_inc(iota_ready, 1)
            pool.wait_ge(xn_stored, 16 * CHUNKS)
            all_groups(pool, lambda st, g: gather(pool, st, g))

        @block.scalar
        def _(act):
            nc.scalar.preload_act_table_set("natural_log_exp_and_others")
            all_chunks(act, chunk_norm)
            act.wait_ge(weights_landed, 32)

            def slot(st, g):
                if g == 0:
                    node(a_s2, act, st, 3)
                    node(a_gex2, act, st, 3)
                if g == 1:
                    node(a_inv2, act, st, 1)
                    node(a_h2, act, st, 3)
                if g == 2:
                    node(a_first, act, st, 2)
                    node(a_topwT, act, st, 3)
                    wait(act, xn2T_done, tiles(st.n - 2))
                    node(a_a1, act, st, 0)
                    node(a_xn2T, act, st, 1)
                    node(a_h2T, act, st, 3)

            act.wait_ge(flag_ready, 1)
            with act.If(act.value_load(ordered[0:1, 0:1], min_val=0, max_val=1) != 0):
                supersteps(act, slot)
            with act.Else():
                node_work(act, [a_a1, a_inv2, a_xn2T, a_first, a_gex2, a_s2, a_h2, a_topwT, a_h2T])

        @block.tensor
        def _(pe):
            pe.wait_ge(ident_ready, 1)
            pe.wait_ge(bad_ready, 1)
            nc.tensor.transpose(p_D[0:1, 0:P], bad[:, 3:4], ident[:]).then_inc(bad_turned, 1)
            pe.wait_ge(weights_landed, 32)

            def slot(st, g):
                if g == 0:
                    wait(pe, y_ready, tiles(st.n - 6))
                    wait(pe, x2_ready, tiles(st.n - 3))
                    node(p_third, pe, st, 4)
                    node(p_l2, pe, st, 1)
                if g == 1:
                    wait(pe, h2T_ready, tiles(st.n - 5))
                    node(p_xnT, pe, st, 0)
                    node(p_first, pe, st, 2)
                if g == 2:
                    wait(pe, a1_ready, tiles(st.n - 2))
                    wait(pe, xn2T_ready, tiles(st.n - 3))
                    wait(pe, h_ready, tiles(st.n - 1))
                    node(p_l1, pe, st, 0)
                    node(p_xn2T, pe, st, 1)
                    node(p_h2T, pe, st, 3)
                edge(edge_aggregate, pe, st, g, 0)
                if g == 1:
                    node(p_topwT, pe, st, 3)
                if g == 2:
                    node(p_second, pe, st, 2)

            def all_windows(st, g):
                J, b = st.group(g)
                with pe.Fori(0, NWIN) as win:
                    pe.wait_ge(rows_landed[b], 16 * KG[g] * (st.i + 1))
                    pe.wait_ge(g_sel_ready, win + (J * NWIN + 1))
                    aggregate(st, g, p_agg[0], g_agg_done)

            pe.wait_ge(flag_ready, 1)
            with pe.If(pe.value_load(ordered[0:1, 0:1], min_val=0, max_val=1) != 0):
                supersteps(pe, slot)
            with pe.Else():
                all_groups(pe, all_windows)
                node_work(pe, [p_xnT, p_l1, p_l2, p_xn2T, p_first, p_second, p_topwT, p_h2T, p_third])

        @block.vector
        def _(dve):
            all_chunks(dve, chunk_stats)
            dve.wait_ge(src_landed, 16)
            for J in range(2 * GROUPS - 1):
                copy_sources(dve, Step(0, J // GROUPS), J % GROUPS)
            dve.wait_ge(base_landed, 16)
            dve.wait_ge(dst_landed, 16)
            dve.wait_ge(iota_ready, 2)
            base3 = base_i[:].rearrange("p (t g) -> p t g", g=GROUPS)
            for g in range(GROUPS):
                s = slice(K0[g], K0[g] + KG[g])
                nc.vector.tensor_tensor(rel[:, 0:T, s], dst_i[:, 0:T, s], base3[:, :, g:g + 1].to_broadcast([P, T, KG[g]]),
                                        ALU.subtract)
            nc.vector.tensor_copy(iota_f[:], iota_i[:])
            nc.vector.tensor_tensor(prog[:], base3, lim_i[:], ALU.subtract).then_inc(dve_const, 1)
            dve.wait_ge(dve_const, 1)
            nc.vector.tensor_reduce(bad[:, 0:1], rel[:, 0:T, :].rearrange("p t k -> p (t k)"), AX_X, ALU.max)
            nc.vector.tensor_reduce(bad[:, 1:2], rel[:, 0:T, :].rearrange("p t k -> p (t k)"), AX_X, ALU.min)
            nc.vector.tensor_reduce(bad[:, 2:3], prog[:].rearrange("p t g -> p (t g)"), AX_X, ALU.min)
            nc.vector.memset(before[:], 0.0)
            nc.vector.memset(onerow[:], 1.0)
            nc.vector.memset(topwT[:], 1.0).then_inc(dve_const, 1)
            dve.wait_ge(dve_const, 2)
            dve.wait_ge(weights_landed, 32)
            for e in range(1, NE):
                nc.vector.memset(before[:, e, 0:e], 1.0)
            e0 = COLS["eps"][0]
            nc.vector.tensor_scalar(eps1[:], wpk[:, e0:e0 + 1], 1.0, None, ALU.add)
            nc.vector.tensor_tensor(bad[:, 1:2], bad[:, 1:2], bad[:, 2:3], ALU.min).then_inc(dve_const, 1)
            dve.wait_ge(dve_const, 3)
            nc.vector.tensor_scalar(bad[:, 1:2], bad[:, 1:2], -1.0, None, ALU.mult)
            nc.vector.tensor_scalar(bad[:, 0:1], bad[:, 0:1], 1.0 - WIN, None, ALU.add).then_inc(dve_const, 1)
            dve.wait_ge(dve_const, 4)
            nc.vector.tensor_tensor(bad[:, 3:4], bad[:, 0:1], bad[:, 1:2], ALU.max).then_inc(bad_ready, 1)
            dve.wait_ge(bad_turned, 1)
            nc.vector.tensor_reduce(badmax[:], p_D[0:1, 0:P], AX_X, ALU.max).then_inc(dve_const, 1)
            dve.wait_ge(dve_const, 5)
            nc.vector.tensor_scalar(ordered[:], badmax[:], 0.0, None, ALU.is_le).then_inc(flag_ready, 1)
            dve.wait_ge(wts_landed, 16)
            dve.wait_ge(xn_stored, 16 * CHUNKS)
            nc.vector.memset(agg[:], 0.0).then_inc(agg_zeroed, 1)
            dve.wait_ge(agg_zeroed, 1)

            def slot(st, g):
                J, b = st.group(g)
                edge(edge_select, dve, st, g, -1)
                edge(sources_ahead, dve, st, g, 0)
                edge(edge_add, dve, st, g, 1)
                if g == 0:
                    node(d_x2, dve, st, 1)
                    node(d_y, dve, st, 4)
                    node(d_gtop, dve, st, 3)
                if g == 1:
                    node(d_xn2, dve, st, 1)
                    adds = J if not isinstance(J, int) else min(J, T * GROUPS)
                    node(d_h, dve, st, 0, lambda eng: eng.wait_ge(added, adds))
                    node(d_gmax, dve, st, 2)
                if g == 2:
                    node(d_gsoft, dve, st, 2)

            def all_windows(st, g):
                J, b = st.group(g)
                K = KG[g]
                if g == 0:
                    wait(dve, rows_used, J)
                    copy_edges(dve, st)
                sources_ahead(dve, st, g)
                wait(dve, rel_ready, st.n + 1)
                wait(dve, g_agg_done, J * NWIN)
                gb = far_base(J)
                nc.vector.tensor_tensor(far[:, 0:K], relc[:, K0[g]:K0[g] + K], gb.to_broadcast([P, K]),
                                        ALU.add).then_inc(far_ready, 1)
                def window(win, first_node, at_end):
                    dve.wait_ge(far_ready, win + (J * NWIN + 1))
                    for k in range(K):
                        last = nc.vector.tensor_scalar(sel[:, g, k, :], iota_f[:], far[:, k:k + 1], wc[:, K0[g] + k:K0[g] + k + 1],
                                                       ALU.is_equal, ALU.mult)
                    last.then_inc(g_sel_ready, 1)
                    dve.wait_ge(g_sel_ready, win + (J * NWIN + 1))
                    if not at_end:
                        nc.vector.tensor_scalar(far[:, 0:K], far[:, 0:K], float(-WIN), None, ALU.add).then_inc(far_ready, 1)
                    dve.wait_ge(g_agg_done, win + (J * NWIN + 1))
                    a = agg[:, :, bass.ds(first_node, WIN)]
                    add = nc.vector.tensor_tensor(a, p_agg[0][:, 0:KD * WIN].rearrange("p (c n) -> p c n", c=KD), a,
                                                  ALU.add)
                    if at_end:
                        add.then_inc(rows_used, 1)
                with dve.Fori(0, NWIN - 1) as win:
                    window(win, win * WIN, False)
                window(NWIN - 1, (NWIN - 1) * WIN, True)
                dve.wait_ge(rows_used, J + 1)

            def far_base(J):
                return base_i[:, bass.ds(J, 1)]

            with dve.If(dve.value_load(ordered[0:1, 0:1], min_val=0, max_val=1) != 0):
                edge_select(dve, Step(0, 0), 0)
                supersteps(dve, slot)
            with dve.Else():
                all_groups(dve, all_windows)
                node_work(dve, [d_h, d_x2, d_xn2, d_gmax, d_gsoft, d_gtop, d_y],
                          lambda eng: eng.wait_ge(rows_used, T * GROUPS))


def kernel(x, src, dst, edge_weight, L0_gnn_eps, L0_gnn_w1, L0_gnn_b1, L0_gnn_w2, L0_gnn_b2,
           L0_ffn_sW1, L0_ffn_sb1, L0_ffn_sW2, L0_ffn_sb2, L0_ffn_sW3, L0_ffn_sb3,
           L0_ffn_eW1, L0_ffn_eb1, L0_ffn_eW2, L0_ffn_eb2, L0_ffn_eW3, L0_ffn_eb3, L0_ffn_gW, L0_ffn_gb):
    import numpy as np
    import concourse.bacc as bacc
    from concourse.bass_utils import run_bass_kernel_spmd

    x, src, dst, edge_weight = (np.asarray(a) for a in (x, src, dst, edge_weight))
    N, E = x.shape[0], src.shape[0]
    T = -(-N // P)
    T += T % 2
    KT = -(-E // (P * T))
    KG = group_tiles(KT)

    def padded(a, n, fill):
        return np.concatenate([a, np.full((n - a.shape[0],) + a.shape[1:], fill, a.dtype)])

    def by_partition(a, fill):
        a = padded(a, T * P * KT, fill).reshape(T, P * KT)
        at, parts = 0, []
        for k in KG:
            parts.append(a[:, at:at + P * k].reshape(T, P, k))
            at += P * k
        return np.concatenate(parts, axis=2), a

    src_t, _ = by_partition(src, 0)
    dst_t, dst_flat = by_partition(dst, dst[-1])
    wts_t, _ = by_partition(edge_weight, 0)
    starts = [P * sum(KG[:g]) for g in range(GROUPS)]
    base = np.broadcast_to(dst_flat[:, starts].reshape(1, -1), (P, T * GROUPS))

    def chunks(a):
        a = np.asarray(a)
        return a.reshape(-1, P, a.shape[1]).transpose(1, 0, 2).reshape(P, -1)

    def column(a):
        return np.asarray(a).reshape(-1, P).T

    eW1 = np.asarray(L0_ffn_eW1)
    packed = np.concatenate([
        chunks(L0_gnn_w1), chunks(L0_gnn_w2), chunks(L0_ffn_sW1), chunks(L0_ffn_sW2), chunks(L0_ffn_sW3),
        eW1.reshape(NE, KD, P, EH1).transpose(2, 1, 0, 3).reshape(P, -1),
        np.asarray(L0_ffn_eW2).transpose(1, 0, 2).reshape(P, -1),
        chunks(np.asarray(L0_ffn_eW3).reshape(NE * EH2, D)), chunks(L0_ffn_gW),
        column(L0_gnn_b1), column(L0_ffn_sb1), column(L0_ffn_sb2), column(L0_ffn_eb1),
        np.broadcast_to(np.asarray(L0_gnn_eps).reshape(1, 1), (P, 1))], axis=1)
    biases = np.concatenate([np.asarray(a).reshape(1, -1) for a in (L0_gnn_b2, L0_ffn_eb2, L0_ffn_gb)], axis=1)
    rows_packed = np.concatenate([
        np.concatenate([np.asarray(L0_ffn_eb3), np.asarray(L0_ffn_sb3).reshape(1, -1)]),
        padded(biases, NE + 1, 0)], axis=1)

    def table(a):
        return padded(a, T + AHEAD, 0).transpose(1, 0, 2).reshape(P, (T + AHEAD) * KT)

    arrays = {"x": padded(x, T * P, 0), "src": table(src_t), "dst": table(dst_t), "weight": table(wts_t),
              "base": base, "packed": packed, "rows_packed": rows_packed}
    arrays = {f"in_{n}": np.ascontiguousarray(a) for n, a in arrays.items()}
    nc = bacc.Bacc("TRN2", target_bir_lowering=False, num_devices=1)
    args = [nc.dram_tensor(n, a.shape, mybir.dt.from_np(a.dtype), kind="ExternalInput").ap() for n, a in arrays.items()]
    xn = nc.dram_tensor("xn", (T * P, D), F32).ap()
    out = nc.dram_tensor("out", (T * P, D), F32, kind="ExternalOutput").ap()
    build(nc, *args, xn, out)
    r = run_bass_kernel_spmd(nc, [arrays], core_ids=[0])
    return r.results[0]["out"][:N]
```

```python
from contextlib import ExitStack

import concourse.bass as bass
from concourse import mybir

ALU = mybir.AluOpType
ACT = mybir.ActivationFunctionType
F32 = mybir.dt.float32
I32 = mybir.dt.int32
AX_X = mybir.AxisListType.X

P = 128
D = 256
KD = D // P
WIN = 64
GROUPS = 3
NE = 4
EH1, EH2 = 128, 64
SH2 = 128
TOPK = 2
LN_EPS = 1e-5
LAG = 2
EARLY = 2
LAST = 3 * 6
PEEL = 3
MAX_CHUNK = 8


def group_tiles(tiles):
    return [(tiles + GROUPS - 1 - g) // GROUPS for g in range(GROUPS)]


def weight_columns():
    at, out = 0, {}
    for name, width in (("w1", KD * D), ("w2", KD * D), ("sW1", KD * D), ("sW2", KD * SH2), ("sW3", D),
                        ("eW1", KD * NE * EH1), ("eW2", NE * EH2), ("eW3", KD * D), ("gW", KD * NE),
                        ("b2", D), ("b1", KD), ("sb1", KD), ("sb2", 1), ("eb1", NE), ("eps", 1)):
        out[name] = (at, width)
        at += width
    return out, at


def build(nc, edges, x, src, dst, weight, base, packed, rows_packed, xn, out):
    T = x.shape[0] // P
    KT = src.shape[1] // T
    KG = group_tiles(KT)
    K0 = [sum(KG[:g]) for g in range(GROUPS)]
    KMAX = max(KG)
    NPAD = T * P + WIN
    NWIN = T * P // WIN
    COLS, WCOLS = weight_columns()
    assert T % 2 == 0 and T // 2 - 1 > PEEL
    LIVE = max(-(-edges // P), (T - 2) * KT + 1)
    R = max(r for r in range(1, MAX_CHUNK + 1) if T // 2 % r == 0 and r < T // 2)
    CHUNKS = T // R

    with ExitStack() as ctx:
        def sb(name, shape, dt=F32):
            return ctx.enter_context(nc.sbuf_tensor(name, shape, dt))

        def bank(name):
            return ctx.enter_context(nc.psum_tensor(name, [P, 512], F32))

        def sem(name):
            return ctx.enter_context(nc.semaphore(name))

        agg = sb("agg", [P, KD, NPAD])
        xs = agg[:].rearrange("p k n -> p (k n)")[:, 0:T * D].rearrange("p (r d) -> p r d", d=D)
        src_i = sb("src_i", [P, T * KT], I32)
        idx = sb("idx", [P, 2, KT], I32)
        rows = sb("rows", [P, 2, KT, D])
        dst_i = sb("dst_i", [P, T, KT], I32)
        rel = dst_i[:].bitcast(F32)
        wts = sb("wts", [P, T * KT])
        base_i = sb("base_i", [P, T * GROUPS], I32)
        prog = sb("prog", [P, T, GROUPS])
        relc = sb("relc", [P, KT])
        wc = sb("wc", [P, KT])
        sel = sb("sel", [P, GROUPS, KMAX, WIN])
        cst6 = sb("cst6", [P, R, 6])
        cwork = sb("cwork", [P, R, 5])
        cnmean = sb("cnmean", [P, 2, R])
        cvar = sb("cvar", [P, 2, R])
        clog = sb("clog", [P, R])
        cinv0 = sb("cinv0", [P, 2, R])
        cnewt = sb("cnewt", [P, 2, R])
        cinv = sb("cinv", [P, 2, R])
        cbias = sb("cbias", [P, 2, R])
        wpk = sb("wpk", [P, WCOLS])
        rpk = sb("rpk", [NE + 1, 2 * D + NE])
        xt = sb("xt", [P, 2, D])
        xnt = sb("xnt", [P, 2, D])
        y = sb("y", [P, 2, D])
        hT = sb("hT", [P, KD, P])
        a1T = sb("a1T", [P, KD, P])
        xn2 = sb("xn2", [P, D])
        xn2T = sb("xn2T", [P, KD, P])
        s1T = sb("s1T", [P, KD, P])
        s2T = sb("s2T", [P, 2, P])
        e1T = sb("e1T", [P, NE, P])
        h2 = sb("h2", [P, D])
        h2T = sb("h2T", [P, KD, P])
        topwT = sb("topwT", [NE + 1, P])
        st6 = sb("st6", [P, 1, 6])
        nwork = sb("nwork", [P, 1, 5])
        nmean = sb("nmean", [P, 2])
        var = sb("var", [P, 2])
        lnv = sb("lnv", [P, 1])
        inv0 = sb("inv0", [P, 2])
        newt = sb("newt", [P, 2])
        inv = sb("inv", [P, 1])
        gmax = sb("gmax", [P, 2])
        gex = sb("gex", [P, NE])
        gsum = sb("gsum", [P, 5])
        gp = sb("gp", [P, NE])
        gex2 = sb("gex2", [P, NE])
        gcmp = sb("gcmp", [P, 3, NE, NE])
        grank = sb("grank", [P, NE])
        gkeep = sb("gkeep", [P, NE])
        topw = sb("topw", [P, NE])
        ident = sb("ident", [P, P])
        onerow = sb("onerow", [1, P])
        zero = sb("zero", [P, 1])
        eps1 = sb("eps1", [P, 1])
        iota_i = sb("iota_i", [P, WIN], I32)
        iota_f = sb("iota_f", [P, WIN])
        lim_i = sb("lim_i", [P, T, GROUPS], I32)
        before = sb("before", [P, NE, NE])
        bad = sb("bad", [P, 4])
        badmax = sb("badmax", [1, 1])
        ordered = sb("ordered", [1, 1], I32)
        far = sb("far", [P, KMAX])

        p_agg = [bank(f"p_agg{n}") for n in range(2)]
        p_A = bank("p_A")
        p_B = bank("p_B")
        p_C = bank("p_C")
        p_D = bank("p_D")
        p_E = bank("p_E")
        p_F = bank("p_F")
        l2_out, ffn_out = p_A[:, 0:D], p_A[:, D:2 * D]
        s1_out, logits = p_B[:, 0:D], p_B[:, D:D + NE]
        xnT_out, h2T_out = p_D[:, 0:D], p_D[:, D:2 * D]
        e2_out, s2_out, topwT_out = p_E[:, 0:D], p_E[:, D:D + SH2], p_E[0:NE, D + SH2:D + SH2 + P]
        l1_out, xn2T_out = p_F[:, 0:D], p_F[:, D:2 * D]

        def w(name, *dims):
            a, n = COLS[name]
            v = wpk[:, a:a + n]
            return v.rearrange("p (k n) -> p k n", k=dims[0]) if dims else v

        w1, w2, sW1, eW3 = (w(n, KD) for n in ("w1", "w2", "sW1", "eW3"))
        sW2, gW = w("sW2", KD), w("gW", KD)
        sW3 = w("sW3")
        eW1 = w("eW1", KD * NE)
        eW2 = w("eW2", NE)
        out_bias = rpk[:, 0:D]
        eb2_row, gb_row = rpk[0:1, D:2 * D], rpk[0:1, 2 * D:2 * D + NE]
        b2 = w("b2")

        rows_landed = [sem(f"rows_landed{n}") for n in range(2 * GROUPS)]
        chunk_landed = [sem(f"chunk_landed{n}") for n in range(2)]
        xn_stored = sem("xn_stored")
        x_landed = [sem(f"x_landed{n}") for n in range(2)]
        xn_landed = [sem(f"xn_landed{n}") for n in range(2)]
        out_stored = [sem(f"out_stored{n}") for n in range(2)]
        src_landed, dst_landed, base_landed = sem("src_landed"), sem("dst_landed"), sem("base_landed")
        weights_landed, wts_landed = sem("weights_landed"), sem("wts_landed")
        rows_turn = sem("rows_turn")
        const_step, ident_ready, iota_ready = sem("const_step"), sem("ident_ready"), sem("iota_ready")
        bad_ready, bad_turned, flag_ready = sem("bad_ready"), sem("bad_turned"), sem("flag_ready")
        dve_const, agg_zeroed = sem("dve_const"), sem("agg_zeroed")
        c_bn, c_mv, c_stats, c_log, c_inv0 = (sem(s) for s in ("c_bn", "c_mv", "c_stats", "c_log", "c_inv0"))
        c_newton = sem("c_newton")
        normed, stats_turn = sem("normed"), sem("stats_turn")
        idx_ready, rel_ready = sem("idx_ready"), sem("rel_ready")
        sel_ready, rows_used, added = sem("sel_ready"), sem("rows_used"), sem("added")
        far_ready, g_sel_ready, g_agg_done = sem("far_ready"), sem("g_sel_ready"), sem("g_agg_done")
        n_bn, n_mv, n_stats, n_log, n_inv0 = (sem(s) for s in ("n_bn", "n_mv", "n_stats", "n_log", "n_inv0"))
        n_newton = sem("n_newton")
        xnT_done, h_ready, l1_done, a1_ready = (sem(s) for s in ("xnT_done", "h_ready", "l1_done", "a1_ready"))
        l2_done, xb_ready, x2_ready = sem("l2_done"), sem("xb_ready"), sem("x2_ready")
        xn2_ready, xn2T_done, xn2T_ready = sem("xn2_ready"), sem("xn2T_done"), sem("xn2T_ready")
        s1_done, e1_done = sem("s1_done"), sem("e1_done")
        gmax_step, gex_ready, gsoft_step = sem("gmax_step"), sem("gex_ready"), sem("gsoft_step")
        gex2_ready, gtop_step = sem("gex2_ready"), sem("gtop_step")
        s1_ready, e1_ready = sem("s1_ready"), sem("e1_ready")
        s2_done, e2_done, s2_ready = sem("s2_done"), sem("e2_done"), sem("s2_ready")
        h2_ready, h2T_done, h2T_ready = sem("h2_ready"), sem("h2T_done"), sem("h2T_ready")
        topwT_done, topwT_ready = sem("topwT_done"), sem("topwT_ready")
        ffn_done, y_ready = sem("ffn_done"), sem("y_ready")
        GSOFT, GTOP = 9, 4

        def wait(eng, s, value):
            if not isinstance(value, int) or value > 0:
                eng.wait_ge(s, value)

        class Step:

            def __init__(self, i, par):
                self.i, self.par = (i + par // 2, par % 2) if par // 2 else (i, par % 2)
                self.n = self.i * 2 + self.par

            def back(self, k):
                return Step(self.i, self.par - k)

            def live(self):
                return not isinstance(self.i, int) or 0 <= self.n < T

            def tiles(self, g):
                if not isinstance(self.i, int):
                    return KG[g]
                return max(0, min(KG[g], LIVE - (self.n * KT + K0[g]))) if 0 <= self.n < T else 0

            def group(self, g):
                return self.n * GROUPS + g, self.par * GROUPS + g

            def landed(self, g):
                return 16 * (KG[g] * self.i + self.tiles(g))

        ALL_GROUPS = sum(Step(t // 2, t % 2).tiles(g) > 0 for t in range(T) for g in range(GROUPS))

        def before_group(st, g, k):
            j = g - k
            return (st.back(-(j // GROUPS)), j % GROUPS)

        def gather(pool, st, g):
            J, b = st.group(g)
            wait(pool, idx_ready, J + 1)
            wait(pool, rows_used, J - 2 * GROUPS + 1)
            pool.sem_inc(rows_turn, 1)
            for k in range(K0[g], K0[g] + st.tiles(g)):
                nc.gpsimd.indirect_dma_start(
                    rows[:, st.par, k, :], None, xn,
                    bass.IndirectOffsetOnAxis(idx[:, st.par, k:k + 1], 0)).then_inc(rows_landed[b], 16)

        def moments(dve, st6_, work, nmean, v, steps, first):
            K = st6_.shape[1]
            halves = st6_.rearrange("p k (h s) -> p k h s", h=2)
            total, lead, square, spread = work[:, 0:K, 0:2], work[:, 0:K, 2], work[:, 0:K, 3], work[:, 0:K, 4]
            nc.vector.tensor_tensor(total, halves[:, :, 0, 1:3], halves[:, :, 1, 1:3], ALU.add)
            nc.vector.tensor_tensor(lead, halves[:, :, 0, 1], halves[:, :, 1, 1], ALU.subtract).then_inc(steps, 1)
            dve.wait_ge(steps, first + 1)
            nc.vector.tensor_scalar(nmean, total[:, :, 0], -0.5, None, ALU.mult)
            nc.vector.scalar_tensor_tensor(out=square, in0=lead, scalar=0.25, in1=lead, op0=ALU.mult, op1=ALU.mult)
            nc.vector.tensor_scalar(spread, total[:, :, 1], 1.0 / D, LN_EPS, ALU.mult, ALU.add).then_inc(steps, 1)
            dve.wait_ge(steps, first + 2)
            return nc.vector.tensor_tensor(v, square, spread, ALU.add)

        def newton(dve, v, y0, new, inv_, steps, first):
            nc.vector.scalar_tensor_tensor(out=new[0], in0=y0, scalar=-0.5, in1=y0,
                                           op0=ALU.mult, op1=ALU.mult).then_inc(steps, 1)
            dve.wait_ge(steps, first + 1)
            nc.vector.tensor_tensor(new[1], new[0], v, ALU.mult).then_inc(steps, 1)
            dve.wait_ge(steps, first + 2)
            nc.vector.scalar_tensor_tensor(out=inv_, in0=new[1], scalar=1.5, in1=y0,
                                           op0=ALU.add, op1=ALU.mult).then_inc(steps, 1)
            dve.wait_ge(steps, first + 3)

        def chunk_rows(c):
            return bass.ds(c.n * R, R)

        def chunk_row(c, r):
            return xs[:, bass.ds(c.n * R + r, 1), :].rearrange("p r d -> p (r d)")

        def chunk_stats(dve, c):
            dve.wait_ge(chunk_landed[c.par], 16 * (c.i + 1))
            dve.sem_inc(stats_turn, 1)
            for r in range(R):
                last = nc.vector.bn_stats(cst6[:, r, :], chunk_row(c, r))
            last.then_inc(c_bn, 1)
            dve.wait_ge(c_bn, c.n + 1)
            wait(dve, c_newton, 4 * (c.n - 1))
            moments(dve, cst6[:], cwork, cnmean[:, c.par, :], cvar[:, c.par, :], c_mv, 2 * c.n).then_inc(c_stats, 1)

        def chunk_inv(dve, c):
            dve.wait_ge(c_inv0, c.n + 1)
            newton(dve, cvar[:, c.par, :], cinv0[:, c.par, :], (cnewt[:, 0, :], cnewt[:, 1, :]), cinv[:, c.par, :],
                   c_newton, 4 * c.n)
            nc.vector.tensor_tensor(cbias[:, c.par, :], cnmean[:, c.par, :], cinv[:, c.par, :], ALU.mult
                                    ).then_inc(c_newton, 1)

        def chunk_inv0(act, c):
            act.wait_ge(c_stats, c.n + 1)
            wait(act, c_inv0, c.n)
            nc.scalar.activation(clog[:], cvar[:, c.par, :], ACT.Ln).then_inc(c_log, 1)
            act.wait_ge(c_log, c.n + 1)
            nc.scalar.activation(cinv0[:, c.par, :], clog[:], ACT.Exp, scale=-0.5).then_inc(c_inv0, 1)

        def chunk_norm(act, c):
            act.wait_ge(c_newton, 4 * c.n + 4)
            for r in range(R):
                row = chunk_row(c, r)
                last = nc.scalar.activation(row, row, ACT.Identity, bias=cbias[:, c.par, r:r + 1],
                                            scale=cinv[:, c.par, r:r + 1])
            last.then_inc(normed, 1)
            act.wait_ge(normed, c.n + 1)
            nc.scalar.dma_start(xn.rearrange("(p r) d -> p r d", p=P)[:, chunk_rows(c), :], xs[:, chunk_rows(c), :]
                                ).then_inc(xn_stored, 16)

        def all_chunks(eng, first, second):
            first(eng, Step(0, 0))
            first(eng, Step(0, 1))
            second(eng, Step(0, 0))
            with eng.Fori(1, CHUNKS // 2) as i:
                for par in range(2):
                    first(eng, Step(i, par))
                    second(eng, Step(i, par).back(1))
            second(eng, Step(CHUNKS // 2 - 1, 1))

        def copy_sources(dve, st, g):
            nc.vector.tensor_copy(idx[:, st.par, K0[g]:K0[g] + KG[g]], src_i[:, bass.ds(st.n * KT + K0[g], KG[g])]
                                  ).then_inc(idx_ready, 1)

        def sources_ahead(dve, st, g):
            J, b = st.group(g)
            s, h = before_group(st, g, 1 - 2 * GROUPS)
            if s.tiles(h):
                wait(dve, rows_used, J)
                copy_sources(dve, s, h)

        def copy_edges(dve, st):
            at = bass.ds(st.n * KT, KT)
            nc.vector.tensor_copy(wc[:], wts[:, at])
            nc.vector.tensor_copy(relc[:], rel.rearrange("p t k -> p (t k)")[:, at]).then_inc(rel_ready, 1)

        def edge_select(dve, st, g):
            J, b = st.group(g)
            if g == 0:
                wait(dve, sel_ready, J)
                copy_edges(dve, st)
            wait(dve, rel_ready, st.n + 1)
            wait(dve, rows_used, J - GROUPS + 1)
            for k in range(K0[g], K0[g] + st.tiles(g)):
                last = nc.vector.tensor_scalar(sel[:, g, k - K0[g], :], iota_f[:], relc[:, k:k + 1], wc[:, k:k + 1],
                                               ALU.is_equal, ALU.mult)
            last.then_inc(sel_ready, 1)

        def aggregate(st, g, bank_, done):
            for c in range(KD):
                for k in range(st.tiles(g)):
                    last = nc.tensor.matmul(bank_[:, c * WIN:(c + 1) * WIN],
                                            rows[:, st.par, K0[g] + k, c * P:(c + 1) * P], sel[:, g, k, :],
                                            start=(k == 0), stop=(k == st.tiles(g) - 1))
            last.then_inc(done, 1)

        def edge_aggregate(pe, st, g):
            J, b = st.group(g)
            pe.wait_ge(sel_ready, J + 1)
            pe.wait_ge(rows_landed[b], st.landed(g))
            wait(pe, added, J - 1)
            aggregate(st, g, p_agg[b % 2], rows_used)

        def edge_add(dve, st, g):
            J, b = st.group(g)
            at = dve.value_load(base_i[0:1, bass.ds(J, 1)], min_val=0, max_val=T * P)
            dve.wait_ge(rows_used, J + 1)
            wait(dve, added, J)
            a = agg[:, :, bass.ds(at, WIN)]
            nc.vector.tensor_tensor(a, p_agg[b % 2][:, 0:KD * WIN].rearrange("p (c n) -> p c n", c=KD), a,
                                    ALU.add).then_inc(added, 1)

        def p_xnT(pe, m):
            pe.wait_ge(xn_landed[m.par], 16 * (m.i + 1))
            wait(pe, h_ready, m.n)
            for c in range(KD):
                last = nc.tensor.transpose(xnT_out[:, c * P:(c + 1) * P], xnt[:, m.par, c * P:(c + 1) * P], ident[:])
            last.then_inc(xnT_done, 1)

        def d_h(dve, m, edges_done):
            dve.wait_ge(xnT_done, m.n + 1)
            edges_done(dve)
            wait(dve, l1_done, m.n)
            nc.vector.scalar_tensor_tensor(out=hT[:], in0=xnT_out.rearrange("p (c n) -> p c n", c=KD), scalar=eps1[:],
                                           in1=tile_of(agg, m), op0=ALU.mult, op1=ALU.add).then_inc(h_ready, 1)

        def tile_of(a, m):
            return a[:, :, bass.ds(m.n * P, P)]

        def p_l1(pe, m):
            pe.wait_ge(h_ready, m.n + 1)
            wait(pe, a1_ready, m.n)
            for o in range(KD):
                for c in range(KD):
                    last = nc.tensor.matmul(l1_out[:, o * P:(o + 1) * P], w1[:, c, o * P:(o + 1) * P], hT[:, c, :],
                                            start=(c == 0), stop=(c == KD - 1))
            last.then_inc(l1_done, 1)

        def a_a1(act, m):
            act.wait_ge(l1_done, m.n + 1)
            wait(act, l2_done, m.n)
            b = COLS["b1"][0]
            for o in range(KD):
                last = nc.scalar.activation(a1T[:, o, :], l1_out[:, o * P:(o + 1) * P], ACT.Relu,
                                            bias=wpk[:, b + o:b + o + 1])
            last.then_inc(a1_ready, 1)

        def p_l2(pe, m):
            pe.wait_ge(a1_ready, m.n + 1)
            wait(pe, x2_ready, m.n)
            for c in range(KD):
                last = nc.tensor.matmul(l2_out, a1T[:, c, :], w2[:, c, :], start=(c == 0), stop=(c == KD - 1))
            last.then_inc(l2_done, 1)

        def d_xb(dve, m):
            dve.wait_ge(x_landed[m.par], 16 * (m.i + 1))
            nc.vector.tensor_tensor(xt[:, m.par, :], xt[:, m.par, :], b2, ALU.add).then_inc(xb_ready, 1)

        def d_x2(dve, m):
            dve.wait_ge(l2_done, m.n + 1)
            dve.wait_ge(xb_ready, m.n + 1)
            dve.wait_ge(h_ready, m.n + 1)
            nc.vector.tensor_tensor(tile_of(agg, m), l2_out.rearrange("p (c n) -> p c n", c=KD),
                                    xt[:, m.par, :].rearrange("p (c n) -> p c n", c=KD), ALU.add).then_inc(x2_ready, 1)
            dve.wait_ge(x2_ready, m.n + 1)
            dve.sem_inc(stats_turn, 1)
            nc.vector.bn_stats(st6[:, 0, :], tile_of(agg, m)).then_inc(n_bn, 1)
            dve.wait_ge(n_bn, m.n + 1)
            moments(dve, st6[:], nwork, nmean[:, m.par:m.par + 1], var[:, m.par:m.par + 1], n_mv, 2 * m.n
                    ).then_inc(n_stats, 1)

        def a_inv2(act, m):
            act.wait_ge(n_stats, m.n + 1)
            wait(act, n_inv0, m.n)
            nc.scalar.activation(lnv[:], var[:, m.par:m.par + 1], ACT.Ln).then_inc(n_log, 1)
            act.wait_ge(n_log, m.n + 1)
            nc.scalar.activation(inv0[:, m.par:m.par + 1], lnv[:], ACT.Exp, scale=-0.5).then_inc(n_inv0, 1)

        def d_xn2(dve, m):
            dve.wait_ge(n_inv0, m.n + 1)
            newton(dve, var[:, m.par:m.par + 1], inv0[:, m.par:m.par + 1], (newt[:, 0:1], newt[:, 1:2]), inv[:],
                   n_newton, 3 * m.n)
            wait(dve, xn2T_done, m.n)
            nc.vector.tensor_scalar(xn2[:].rearrange("p (c n) -> p c n", c=KD), tile_of(agg, m),
                                    nmean[:, m.par:m.par + 1], inv[:], ALU.add, ALU.mult).then_inc(xn2_ready, 1)

        def p_xn2T(pe, m):
            pe.wait_ge(xn2_ready, m.n + 1)
            wait(pe, xn2T_ready, m.n)
            for c in range(KD):
                last = nc.tensor.transpose(xn2T_out[:, c * P:(c + 1) * P], xn2[:, c * P:(c + 1) * P], ident[:])
            last.then_inc(xn2T_done, 1)

        def a_xn2T(act, m):
            act.wait_ge(xn2T_done, m.n + 1)
            wait(act, e1_done, m.n)
            nc.scalar.copy(xn2T[:].rearrange("p c n -> p (c n)"), xn2T_out).then_inc(xn2T_ready, 1)

        def p_first(pe, m):
            pe.wait_ge(xn2T_ready, m.n + 1)
            wait(pe, s1_ready, m.n)
            for c in range(KD):
                nc.tensor.matmul(logits, xn2T[:, c, :], gW[:, c, :], start=(c == 0), stop=False)
            nc.tensor.matmul(logits, onerow[:], gb_row, start=False, stop=True)
            for o in range(KD):
                for c in range(KD):
                    last = nc.tensor.matmul(s1_out[:, o * P:(o + 1) * P], sW1[:, c, o * P:(o + 1) * P], xn2T[:, c, :],
                                            start=(c == 0), stop=(c == KD - 1))
            last.then_inc(s1_done, 1)
            wait(pe, e1_ready, m.n)
            for e in range(NE):
                for c in range(KD):
                    last = nc.tensor.matmul(p_C[:, e * P:(e + 1) * P], eW1[:, c * NE + e, :], xn2T[:, c, :],
                                            start=(c == 0), stop=(c == KD - 1))
            last.then_inc(e1_done, 1)

        def d_gmax(dve, m):
            dve.wait_ge(s1_done, m.n + 1)
            nc.vector.tensor_reduce(gmax[:, 0:1], logits, AX_X, ALU.max).then_inc(gmax_step, 1)
            dve.wait_ge(gmax_step, 2 * m.n + 1)
            nc.vector.tensor_scalar(gmax[:, 1:2], gmax[:, 0:1], -1.0, None, ALU.mult).then_inc(gmax_step, 1)

        def a_first(act, m):
            act.wait_ge(gmax_step, 2 * m.n + 2)
            nc.scalar.activation(gex[:], logits, ACT.Exp, bias=gmax[:, 1:2]).then_inc(gex_ready, 1)
            act.wait_ge(s1_done, m.n + 1)
            wait(act, s2_done, m.n)
            b = COLS["sb1"][0]
            for o in range(KD):
                last = nc.scalar.activation(s1T[:, o, :], s1_out[:, o * P:(o + 1) * P], ACT.Relu,
                                            bias=wpk[:, b + o:b + o + 1])
            last.then_inc(s1_ready, 1)
            act.wait_ge(e1_done, m.n + 1)
            wait(act, e2_done, m.n)
            b = COLS["eb1"][0]
            for e in range(NE):
                last = nc.scalar.activation(e1T[:, e, :], p_C[:, e * P:(e + 1) * P], ACT.Relu,
                                            bias=wpk[:, b + e:b + e + 1])
            last.then_inc(e1_ready, 1)

        def p_second(pe, m):
            pe.wait_ge(s1_ready, m.n + 1)
            wait(pe, topwT_ready, m.n)
            for c in range(KD):
                last = nc.tensor.matmul(s2_out, sW2[:, c, :], s1T[:, c, :], start=(c == 0), stop=(c == KD - 1))
            last.then_inc(s2_done, 1)
            pe.wait_ge(e1_ready, m.n + 1)
            for e in range(NE):
                o = e2_out[:, e * EH2:(e + 1) * EH2]
                nc.tensor.matmul(o, e1T[:, e, :], eW2[:, e, :], start=True, stop=False)
                last = nc.tensor.matmul(o, onerow[:], eb2_row[:, e * EH2:(e + 1) * EH2], start=False, stop=True)
            last.then_inc(e2_done, 1)

        def a_s2(act, m):
            act.wait_ge(e2_done, m.n + 1)
            wait(act, ffn_done, m.n - 1)
            b = COLS["sb2"][0]
            nc.scalar.activation(s2T[:, m.par, :], s2_out, ACT.Relu, bias=wpk[:, b:b + 1]).then_inc(s2_ready, 1)

        def d_gsoft(dve, m):
            n = [GSOFT * m.n]
            by_row = gp[:].unsqueeze(1).to_broadcast([P, NE, NE])
            by_col = gp[:].unsqueeze(2).to_broadcast([P, NE, NE])

            def step(ins):
                ins.then_inc(gsoft_step, 1)
                n[0] = n[0] + 1
                dve.wait_ge(gsoft_step, n[0])

            dve.wait_ge(gex_ready, m.n + 1)
            step(nc.vector.reduce_sum(gsum[:, 0:1], gex[:], AX_X))
            step(nc.vector.reciprocal(gsum[:, 1:2], gsum[:, 0:1]))
            step(nc.vector.tensor_scalar(gp[:], gex[:], gsum[:, 1:2], None, ALU.mult))
            step(nc.vector.tensor_scalar(gsum[:, 2:3], gsum[:, 1:2], -1.0, None, ALU.mult))
            step(nc.vector.tensor_tensor(gcmp[:, 0], by_row, by_col, ALU.is_gt))
            step(nc.vector.tensor_tensor(gcmp[:, 1], by_row, by_col, ALU.is_equal))
            step(nc.vector.tensor_tensor(gcmp[:, 2], gcmp[:, 1], before[:], ALU.mult))
            step(nc.vector.tensor_tensor(gcmp[:, 1], gcmp[:, 2], gcmp[:, 0], ALU.add))
            step(nc.vector.tensor_reduce(grank[:], gcmp[:, 1], AX_X, ALU.add))

        def a_gex2(act, m):
            act.wait_ge(gsoft_step, GSOFT * m.n + 4)
            wait(act, gtop_step, GTOP * m.n)
            nc.scalar.activation(gex2[:], gp[:], ACT.Exp, bias=gsum[:, 2:3]).then_inc(gex2_ready, 1)

        def d_gtop(dve, m):
            dve.wait_ge(gex2_ready, m.n + 1)
            wait(dve, topwT_done, m.n)
            n = GTOP * m.n
            nc.vector.scalar_tensor_tensor(out=gkeep[:], in0=grank[:], scalar=TOPK - 0.5, in1=gex2[:],
                                           op0=ALU.is_lt, op1=ALU.mult).then_inc(gtop_step, 1)
            dve.wait_ge(gtop_step, n + 1)
            nc.vector.reduce_sum(gsum[:, 3:4], gkeep[:], AX_X).then_inc(gtop_step, 1)
            dve.wait_ge(gtop_step, n + 2)
            nc.vector.reciprocal(gsum[:, 4:5], gsum[:, 3:4]).then_inc(gtop_step, 1)
            dve.wait_ge(gtop_step, n + 3)
            nc.vector.tensor_scalar(topw[:], gkeep[:], gsum[:, 4:5], None, ALU.mult).then_inc(gtop_step, 1)

        def a_h2(act, m):
            act.wait_ge(e2_done, m.n + 1)
            act.wait_ge(gtop_step, GTOP * m.n + GTOP)
            wait(act, h2T_done, m.n)
            for e in range(NE):
                s = slice(e * EH2, (e + 1) * EH2)
                last = nc.scalar.activation(h2[:, s], e2_out[:, s], ACT.Relu, scale=topw[:, e:e + 1])
            last.then_inc(h2_ready, 1)

        def p_topwT(pe, m):
            pe.wait_ge(gtop_step, GTOP * m.n + GTOP)
            pe.wait_ge(s2_ready, m.n + 1)
            pe.wait_ge(h2_ready, m.n + 1)
            nc.tensor.transpose(topwT_out, topw[:], ident[:]).then_inc(topwT_done, 1)

        def p_h2T(pe, m):
            pe.wait_ge(h2_ready, m.n + 1)
            wait(pe, h2T_ready, m.n)
            for c in range(KD):
                last = nc.tensor.transpose(h2T_out[:, c * P:(c + 1) * P], h2[:, c * P:(c + 1) * P], ident[:])
            last.then_inc(h2T_done, 1)

        def a_topwT(act, m):
            act.wait_ge(topwT_done, m.n + 1)
            wait(act, ffn_done, m.n)
            if isinstance(m.n, int) and m.n == 0:
                act.wait_ge(dve_const, 4)
            nc.scalar.copy(topwT[0:NE, :], topwT_out).then_inc(topwT_ready, 1)

        def a_h2T(act, m):
            act.wait_ge(h2T_done, m.n + 1)
            wait(act, ffn_done, m.n)
            nc.scalar.copy(h2T[:].rearrange("p c n -> p (c n)"), h2T_out).then_inc(h2T_ready, 1)

        def p_third(pe, m):
            wait(pe, y_ready, m.n)
            pe.wait_ge(s2_ready, m.n + 1)
            nc.tensor.matmul(ffn_out, s2T[:, m.par, :], sW3, start=True, stop=False)
            pe.wait_ge(topwT_ready, m.n + 1)
            nc.tensor.matmul(ffn_out, topwT[:], out_bias, start=False, stop=False)
            pe.wait_ge(h2T_ready, m.n + 1)
            for c in range(KD):
                last = nc.tensor.matmul(ffn_out, h2T[:, c, :], eW3[:, c, :], start=False, stop=(c == KD - 1))
            last.then_inc(ffn_done, 1)

        def d_y(dve, m):
            dve.wait_ge(ffn_done, m.n + 1)
            wait(dve, out_stored[m.par], 16 * m.i)
            nc.vector.tensor_tensor(y[:, m.par, :].rearrange("p (c n) -> p c n", c=KD),
                                    ffn_out.rearrange("p (c n) -> p c n", c=KD), tile_of(agg, m), ALU.add
                                    ).then_inc(y_ready, 1)

        def supersteps(eng, slot):
            def slots(first, last):
                for J in range(first, last):
                    t = J // GROUPS
                    slot(Step(t // 2, t % 2), J % GROUPS)

            slots(0, 2 * PEEL * GROUPS)
            with eng.Fori(PEEL, T // 2 - 1) as i:
                for par in range(2):
                    for g in range(GROUPS):
                        slot(Step(i, par), g)
            slots((T - 2) * GROUPS, (T - 1) * GROUPS + LAST - EARLY + 1)

        def node(stage, eng, st, later, *more):
            m = st.back(LAG + later)
            if m.live():
                stage(eng, m, *more)

        def tiles(n):
            return min(n, T) if isinstance(n, int) else n

        def edge(stage, eng, st, g, earlier):
            s, h = before_group(st, g, earlier)
            if s.tiles(h):
                stage(eng, s, h)

        def node_work(eng, stages, edges_done=None):
            def tile_(m):
                for stage in stages:
                    if stage is d_h:
                        stage(eng, m, edges_done)
                    else:
                        stage(eng, m)
            for par in range(2):
                tile_(Step(0, par))
            with eng.Fori(1, T // 2) as i:
                for par in range(2):
                    tile_(Step(i, par))

        def all_groups(eng, body):
            def pair(i):
                for par in range(2):
                    for g in range(GROUPS):
                        if Step(i, par).tiles(g):
                            body(Step(i, par), g)

            pair(0)
            with eng.Fori(1, T // 2 - 1) as i:
                pair(i)
            pair(T // 2 - 1)

        block = ctx.enter_context(nc.Block())

        @block.sync
        def _(sp):
            def load_chunk(c):
                wait(sp, chunk_landed[c.par], 16 * c.i)
                sp.dma_start(xs[:, chunk_rows(c), :], x.rearrange("(p r) d -> p r d", p=P)[:, chunk_rows(c), :]
                             ).then_inc(chunk_landed[c.par], 16)

            def load_xn(m):
                wait(sp, xnT_done, m.n - 1)
                sp.dma_start(xnt[:, m.par, :], xn[bass.ds(m.n * P, P), :]).then_inc(xn_landed[m.par], 16)

            def load_x(m):
                wait(sp, x2_ready, m.n - 1)
                sp.dma_start(xt[:, m.par, :], x[bass.ds(m.n * P, P), :]).then_inc(x_landed[m.par], 16)

            def store(m):
                sp.wait_ge(y_ready, m.n + 1)
                sp.dma_start(out[bass.ds(m.n * P, P), :], y[:, m.par, :]).then_inc(out_stored[m.par], 16)

            for par in range(2):
                load_chunk(Step(0, par))
            with sp.Fori(1, CHUNKS // 2) as i:
                for par in range(2):
                    load_chunk(Step(i, par))
            sp.dma_start(src_i[:], src).then_inc(src_landed, 16)
            sp.wait_ge(xn_stored, 16 * CHUNKS)
            sp.dma_start(dst_i[:].rearrange("p t k -> p (t k)"), dst).then_inc(dst_landed, 16)
            sp.dma_start(base_i[:], base).then_inc(base_landed, 16)
            sp.dma_start(wts[:], weight).then_inc(wts_landed, 16)
            sp.dma_start(wpk[:], packed).then_inc(weights_landed, 16)
            sp.dma_start(rpk[:], rows_packed).then_inc(weights_landed, 16)

            def serve(m, first=False):
                load_xn(m)
                if not first:
                    load_x(m.back(1))

            serve(Step(0, 0), True)
            for m in range(1, 4):
                serve(Step(m // 2, m % 2))
            with sp.Fori(2, T // 2) as i:
                for par in range(2):
                    serve(Step(i, par))
                    store(Step(i - 2, par))
            load_x(Step(T // 2 - 1, 1))
            for i in range(T // 2 - 2, T // 2):
                for par in range(2):
                    store(Step(i, par))
            for par in range(2):
                sp.wait_ge(out_stored[par], 16 * (T // 2))

        @block.gpsimd
        def _(pool):
            nc.gpsimd.memset(ident[:], 0.0).then_inc(const_step, 1)
            pool.wait_ge(const_step, 1)
            nc.gpsimd.affine_select(out=ident[:], in_=ident[:], compare_op=ALU.not_equal, fill=1.0, base=0,
                                    pattern=[[-1, P]], channel_multiplier=1).then_inc(ident_ready, 1)
            nc.gpsimd.iota(iota_i[:], pattern=[[1, WIN]], base=0, channel_multiplier=0).then_inc(iota_ready, 1)
            for g in range(GROUPS):
                nc.gpsimd.iota(lim_i[:, :, g:g + 1], pattern=[[P, T], [0, 1]], base=0 if g >= GROUPS + 1 - EARLY else -P,
                               channel_multiplier=0).then_inc(iota_ready, 1)
            pool.wait_ge(xn_stored, 16 * CHUNKS)
            all_groups(pool, lambda st, g: gather(pool, st, g))

        @block.scalar
        def _(act):
            nc.scalar.preload_act_table_set("natural_log_exp_and_others")
            all_chunks(act, chunk_inv0, chunk_norm)
            act.wait_ge(dve_const, 1)
            act.wait_ge(xn_stored, 16 * CHUNKS)
            nc.scalar.copy(agg[:, 1:KD, :], zero[:].unsqueeze(2).to_broadcast([P, KD - 1, NPAD])
                           ).then_inc(agg_zeroed, 1)
            act.wait_ge(weights_landed, 32)

            def slot(st, g):
                st, g = before_group(st, g, -EARLY)
                if g == 0:
                    node(a_s2, act, st, 3)
                    node(a_gex2, act, st, 3)
                if g == 1:
                    node(a_inv2, act, st, 1)
                    node(a_h2, act, st, 3)
                if g == 2:
                    node(a_first, act, st, 2)
                    node(a_topwT, act, st, 3)
                    wait(act, xn2T_done, tiles(st.n - 2))
                    node(a_a1, act, st, 0)
                    node(a_xn2T, act, st, 1)
                    node(a_h2T, act, st, 3)

            act.wait_ge(flag_ready, 1)
            with act.If(act.value_load(ordered[0:1, 0:1], min_val=0, max_val=1) != 0):
                supersteps(act, slot)
            with act.Else():
                node_work(act, [a_a1, a_inv2, a_xn2T, a_first, a_gex2, a_s2, a_h2, a_topwT, a_h2T])

        @block.tensor
        def _(pe):
            pe.wait_ge(ident_ready, 1)
            pe.wait_ge(bad_ready, 1)
            nc.tensor.transpose(p_D[0:1, 0:P], bad[:, 3:4], ident[:]).then_inc(bad_turned, 1)
            pe.wait_ge(weights_landed, 32)

            def slot(edge_st, edge_g):
                st, g = before_group(edge_st, edge_g, -EARLY)
                if g == 0:
                    wait(pe, y_ready, tiles(st.n - 6))
                    wait(pe, x2_ready, tiles(st.n - 3))
                    node(p_third, pe, st, 4)
                    node(p_l2, pe, st, 1)
                if g == 1:
                    wait(pe, h2T_ready, tiles(st.n - 5))
                    node(p_xnT, pe, st, 0)
                    node(p_first, pe, st, 2)
                if g == 2:
                    wait(pe, a1_ready, tiles(st.n - 2))
                    wait(pe, xn2T_ready, tiles(st.n - 3))
                    wait(pe, h_ready, tiles(st.n - 1))
                    node(p_l1, pe, st, 0)
                    node(p_xn2T, pe, st, 1)
                    node(p_h2T, pe, st, 3)
                edge(edge_aggregate, pe, edge_st, edge_g, 0)
                if g == 1:
                    node(p_topwT, pe, st, 3)
                if g == 2:
                    node(p_second, pe, st, 2)

            def all_windows(st, g):
                J, b = st.group(g)
                with pe.Fori(0, NWIN) as win:
                    pe.wait_ge(rows_landed[b], st.landed(g))
                    pe.wait_ge(g_sel_ready, win + (J * NWIN + 1))
                    aggregate(st, g, p_agg[0], g_agg_done)

            pe.wait_ge(flag_ready, 1)
            with pe.If(pe.value_load(ordered[0:1, 0:1], min_val=0, max_val=1) != 0):
                supersteps(pe, slot)
            with pe.Else():
                all_groups(pe, all_windows)
                node_work(pe, [p_xnT, p_l1, p_l2, p_xn2T, p_first, p_second, p_topwT, p_h2T, p_third])

        @block.vector
        def _(dve):
            nc.vector.memset(zero[:], 0.0).then_inc(dve_const, 1)
            all_chunks(dve, chunk_stats, chunk_inv)
            dve.wait_ge(src_landed, 16)
            for J in range(2 * GROUPS - 1):
                copy_sources(dve, Step(0, J // GROUPS), J % GROUPS)
            dve.wait_ge(xn_stored, 16 * CHUNKS)
            nc.vector.memset(agg[:, 0:1, :], 0.0).then_inc(agg_zeroed, 1)
            dve.wait_ge(base_landed, 16)
            dve.wait_ge(dst_landed, 16)
            dve.wait_ge(iota_ready, 1 + GROUPS)
            base3 = base_i[:].rearrange("p (t g) -> p t g", g=GROUPS)
            for g in range(GROUPS):
                s = slice(K0[g], K0[g] + KG[g])
                nc.vector.tensor_tensor(rel[:, :, s], dst_i[:, :, s], base3[:, :, g:g + 1].to_broadcast([P, T, KG[g]]),
                                        ALU.subtract)
            nc.vector.tensor_copy(iota_f[:], iota_i[:])
            nc.vector.tensor_tensor(prog[:], base3, lim_i[:], ALU.subtract).then_inc(dve_const, 1)
            dve.wait_ge(dve_const, 2)
            nc.vector.tensor_reduce(bad[:, 0:1], rel.rearrange("p t k -> p (t k)"), AX_X, ALU.max)
            nc.vector.tensor_reduce(bad[:, 1:2], rel.rearrange("p t k -> p (t k)"), AX_X, ALU.min)
            nc.vector.tensor_reduce(bad[:, 2:3], prog[:].rearrange("p t g -> p (t g)"), AX_X, ALU.min)
            nc.vector.memset(before[:], 0.0)
            nc.vector.memset(onerow[:], 1.0)
            nc.vector.memset(topwT[:], 1.0).then_inc(dve_const, 1)
            dve.wait_ge(dve_const, 3)
            dve.wait_ge(weights_landed, 32)
            for e in range(1, NE):
                nc.vector.memset(before[:, e, 0:e], 1.0)
            e0 = COLS["eps"][0]
            nc.vector.tensor_scalar(eps1[:], wpk[:, e0:e0 + 1], 1.0, None, ALU.add)
            nc.vector.tensor_tensor(bad[:, 1:2], bad[:, 1:2], bad[:, 2:3], ALU.min).then_inc(dve_const, 1)
            dve.wait_ge(dve_const, 4)
            nc.vector.tensor_scalar(bad[:, 1:2], bad[:, 1:2], -1.0, None, ALU.mult)
            nc.vector.tensor_scalar(bad[:, 0:1], bad[:, 0:1], 1.0 - WIN, None, ALU.add).then_inc(dve_const, 1)
            dve.wait_ge(dve_const, 5)
            nc.vector.tensor_tensor(bad[:, 3:4], bad[:, 0:1], bad[:, 1:2], ALU.max).then_inc(bad_ready, 1)
            dve.wait_ge(bad_turned, 1)
            nc.vector.tensor_reduce(badmax[:], p_D[0:1, 0:P], AX_X, ALU.max).then_inc(dve_const, 1)
            dve.wait_ge(dve_const, 6)
            nc.vector.tensor_scalar(ordered[:], badmax[:], 0.0, None, ALU.is_le).then_inc(flag_ready, 1)
            dve.wait_ge(agg_zeroed, 2)
            dve.wait_ge(wts_landed, 16)
            dve.wait_ge(flag_ready, 1)

            def slot(st, g):
                J, b = st.group(g)
                edge(edge_select, dve, st, g, -1)
                edge(sources_ahead, dve, st, g, 0)
                edge(edge_add, dve, st, g, 1)
                st, g = before_group(st, g, -EARLY)
                if g == 0:
                    node(d_x2, dve, st, 1)
                    node(d_y, dve, st, 4)
                    node(d_gtop, dve, st, 3)
                if g == 1:
                    node(d_xn2, dve, st, 1)
                    adds = J if not isinstance(J, int) else min(J, ALL_GROUPS)
                    node(d_h, dve, st, 0, lambda eng: eng.wait_ge(added, adds))
                    node(d_gmax, dve, st, 2)
                if g == 2:
                    node(d_xb, dve, st, 0)
                    node(d_gsoft, dve, st, 2)

            def all_windows(st, g):
                J, b = st.group(g)
                K = KG[g]
                if g == 0:
                    wait(dve, rows_used, J)
                    copy_edges(dve, st)
                sources_ahead(dve, st, g)
                wait(dve, rel_ready, st.n + 1)
                wait(dve, g_agg_done, J * NWIN)
                gb = far_base(J)
                nc.vector.tensor_tensor(far[:, 0:K], relc[:, K0[g]:K0[g] + K], gb.to_broadcast([P, K]),
                                        ALU.add).then_inc(far_ready, 1)
                def window(win, first_node, at_end):
                    dve.wait_ge(far_ready, win + (J * NWIN + 1))
                    for k in range(K):
                        last = nc.vector.tensor_scalar(sel[:, g, k, :], iota_f[:], far[:, k:k + 1],
                                                       wc[:, K0[g] + k:K0[g] + k + 1],
                                                       ALU.is_equal, ALU.mult)
                    last.then_inc(g_sel_ready, 1)
                    dve.wait_ge(g_sel_ready, win + (J * NWIN + 1))
                    if not at_end:
                        nc.vector.tensor_scalar(far[:, 0:K], far[:, 0:K], float(-WIN), None, ALU.add).then_inc(far_ready, 1)
                    dve.wait_ge(g_agg_done, win + (J * NWIN + 1))
                    a = agg[:, :, bass.ds(first_node, WIN)]
                    add = nc.vector.tensor_tensor(a, p_agg[0][:, 0:KD * WIN].rearrange("p (c n) -> p c n", c=KD), a,
                                                  ALU.add)
                    if at_end:
                        add.then_inc(rows_used, 1)
                with dve.Fori(0, NWIN - 1) as win:
                    window(win, win * WIN, False)
                window(NWIN - 1, (NWIN - 1) * WIN, True)
                dve.wait_ge(rows_used, J + 1)

            def far_base(J):
                return base_i[:, bass.ds(J, 1)]

            with dve.If(dve.value_load(ordered[0:1, 0:1], min_val=0, max_val=1) != 0):
                edge_select(dve, Step(0, 0), 0)
                supersteps(dve, slot)
            with dve.Else():
                all_groups(dve, all_windows)
                node_work(dve, [d_h, d_xb, d_x2, d_xn2, d_gmax, d_gsoft, d_gtop, d_y],
                          lambda eng: eng.wait_ge(rows_used, ALL_GROUPS))


def kernel(x, src, dst, edge_weight, L0_gnn_eps, L0_gnn_w1, L0_gnn_b1, L0_gnn_w2, L0_gnn_b2,
           L0_ffn_sW1, L0_ffn_sb1, L0_ffn_sW2, L0_ffn_sb2, L0_ffn_sW3, L0_ffn_sb3,
           L0_ffn_eW1, L0_ffn_eb1, L0_ffn_eW2, L0_ffn_eb2, L0_ffn_eW3, L0_ffn_eb3, L0_ffn_gW, L0_ffn_gb):
    import numpy as np
    import concourse.bacc as bacc
    from concourse.bass_utils import run_bass_kernel_spmd

    x, src, dst, edge_weight = (np.asarray(a) for a in (x, src, dst, edge_weight))
    N, E = x.shape[0], src.shape[0]
    T = -(-N // P)
    T += T % 2
    KT = -(-E // (P * T))
    KG = group_tiles(KT)

    def padded(a, n, fill):
        return np.concatenate([a, np.full((n - a.shape[0],) + a.shape[1:], fill, a.dtype)])

    def by_partition(a, fill):
        a = padded(a, T * P * KT, fill).reshape(T, P * KT)
        return a.reshape(T, KT, P).transpose(0, 2, 1), a

    src_t, _ = by_partition(src, 0)
    dst_t, dst_flat = by_partition(dst, dst[-1])
    wts_t, _ = by_partition(edge_weight, 0)
    starts = [P * sum(KG[:g]) for g in range(GROUPS)]
    base = np.broadcast_to(dst_flat[:, starts].reshape(1, -1), (P, T * GROUPS))

    def chunks(a):
        a = np.asarray(a)
        return a.reshape(-1, P, a.shape[1]).transpose(1, 0, 2).reshape(P, -1)

    def column(a):
        return np.asarray(a).reshape(-1, P).T

    eW1 = np.asarray(L0_ffn_eW1)
    packed = np.concatenate([
        chunks(L0_gnn_w1), chunks(L0_gnn_w2), chunks(L0_ffn_sW1), chunks(L0_ffn_sW2), chunks(L0_ffn_sW3),
        eW1.reshape(NE, KD, P, EH1).transpose(2, 1, 0, 3).reshape(P, -1),
        np.asarray(L0_ffn_eW2).transpose(1, 0, 2).reshape(P, -1),
        chunks(np.asarray(L0_ffn_eW3).reshape(NE * EH2, D)), chunks(L0_ffn_gW),
        np.broadcast_to(np.asarray(L0_gnn_b2).reshape(1, D), (P, D)),
        column(L0_gnn_b1), column(L0_ffn_sb1), column(L0_ffn_sb2), column(L0_ffn_eb1),
        np.broadcast_to(np.asarray(L0_gnn_eps).reshape(1, 1), (P, 1))], axis=1)
    biases = np.concatenate([np.asarray(a).reshape(1, -1) for a in (L0_ffn_eb2, L0_ffn_gb)], axis=1)
    rows_packed = np.concatenate([
        np.concatenate([np.asarray(L0_ffn_eb3), np.asarray(L0_ffn_sb3).reshape(1, -1)]),
        padded(biases, NE + 1, 0)], axis=1)

    def table(a):
        return a.transpose(1, 0, 2).reshape(P, T * KT)

    arrays = {"x": padded(x, T * P, 0), "src": table(src_t), "dst": table(dst_t), "weight": table(wts_t),
              "base": base, "packed": packed, "rows_packed": rows_packed}
    arrays = {f"in_{n}": np.ascontiguousarray(a) for n, a in arrays.items()}
    nc = bacc.Bacc("TRN2", target_bir_lowering=False, num_devices=1)
    args = [nc.dram_tensor(n, a.shape, mybir.dt.from_np(a.dtype), kind="ExternalInput").ap() for n, a in arrays.items()]
    xn = nc.dram_tensor("xn", (T * P, D), F32).ap()
    out = nc.dram_tensor("out", (T * P, D), F32, kind="ExternalOutput").ap()
    build(nc, E, *args, xn, out)
    r = run_bass_kernel_spmd(nc, [arrays], core_ids=[0])
    return r.results[0]["out"][:N]
```
